# Optimizing a Trainium2 kernel written in Bass

```python
import numpy as np
import jax
import jax.numpy as jnp

def _softmax(x, axis=-1):
    return jax.nn.softmax(x, axis=axis)

def _gelu(x):
    return jax.nn.gelu(x, approximate=True)

def _silu(x):
    return jax.nn.silu(x)

def _sigmoid(x):
    return jax.nn.sigmoid(x)

def _layernorm(x, axis=-1, eps=1e-05):
    m = jnp.mean(x, axis=axis, keepdims=True)
    v = jnp.var(x, axis=axis, keepdims=True)
    return (x - m) / jnp.sqrt(v + eps)

def _scatter_add(tgt, idx, src, axis=0):
    return tgt.at[idx].add(src)

def _segment_sum(src, seg, n):
    return jax.ops.segment_sum(src, seg, n)
kernel_name = 'mk_xattn_ffn_d2_seqx_r4_863cbe'

def setup_inputs(seed: int=0):
    np.random.seed(seed)
    _w = jnp.asarray

    def _rec_inputs():
        import jax
        import jax.numpy as jnp
        _rk = jax.random.key(seed)
        x = -0.0002928 + 1 * jax.random.normal(jax.random.fold_in(_rk, 1), (4, 1024, 256), jnp.float32)
        _lenS = 1024 - jax.random.randint(jax.random.fold_in(_rk, 7), (4,), 0, max(1, 1024 // 4) + 1, jnp.int32)
        _lenS2 = 64 - jax.random.randint(jax.random.fold_in(_rk, 8), (4,), 0, max(1, 64 // 4) + 1, jnp.int32)
        _ctx_1024P = jax.random.normal(jax.random.fold_in(_rk, 11), (4, 16, 256), jnp.float32)
        _ctx_1024c = jax.random.dirichlet(jax.random.fold_in(_rk, 511), 0.3 * jnp.ones((16,), jnp.float32), (4, 64))
        _ctx_1024t = jnp.einsum('bsk,bkd->bsd', _ctx_1024c, _ctx_1024P)
        _ctx_1024t = _ctx_1024t * jax.lax.rsqrt(jnp.mean(jnp.square(_ctx_1024t)) + 1e-12) * 0.953939
        ctx_1024 = 2.81802e-05 + 1.00001 * (_ctx_1024t + 0.3 * jax.random.normal(jax.random.fold_in(_rk, 611), (4, 64, 256), jnp.float32))
        fside_BxSxS2_0 = jax.random.uniform(jax.random.fold_in(_rk, 12), (4, 1024, 64), jnp.float32, 0.0, 1)
        _validS = jnp.arange(1024)[None, :] < _lenS[:, None]
        _validS2 = jnp.arange(64)[None, :] < _lenS2[:, None]
        _causal = jnp.tril(jnp.ones((1024, 1024), dtype=bool))
        mask_BxSxS2_ik1 = jnp.where(jnp.broadcast_to(_validS2[:, None, :], (4, 1024, 64)), 1, 0).astype(jnp.int32)
        return (x, ctx_1024, fside_BxSxS2_0, mask_BxSxS2_ik1)
    x, ctx_1024, fside_BxSxS2_0, mask_BxSxS2_ik1 = _rec_inputs()

    def _L0_xattn_setup():
        import jax, jax.numpy as jnp
        import numpy as np
        B, T, S, DIN, H = (64, 64, 64, 256, 256)
        SCALE = 0.02

        def _lstm_cell(x, h, c, Wi, Wh, bi, bh):
            g = x @ Wi.T + bi + h @ Wh.T + bh
            i, f, gg, o = jnp.split(g, 4, axis=-1)
            c2 = jax.nn.sigmoid(f) * c + jax.nn.sigmoid(i) * jnp.tanh(gg)
            h2 = jax.nn.sigmoid(o) * jnp.tanh(c2)
            return (h2, c2)
        key = jax.random.key(seed)
        ks = jax.random.split(key, 12)
        n = jax.random.normal
        return {'inputs': n(ks[0], (B, T, DIN), jnp.float32), 'context': n(ks[1], (B, S, H), jnp.float32), 'Wi0': n(ks[2], (4 * H, DIN + H), jnp.float32) * SCALE, 'Wh0': n(ks[3], (4 * H, H), jnp.float32) * SCALE, 'bi0': jnp.zeros((4 * H,), jnp.float32), 'bh0': jnp.zeros((4 * H,), jnp.float32), 'Wi1': n(ks[4], (4 * H, H), jnp.float32) * SCALE, 'Wh1': n(ks[5], (4 * H, H), jnp.float32) * SCALE, 'bi1': jnp.zeros((4 * H,), jnp.float32), 'bh1': jnp.zeros((4 * H,), jnp.float32), 'Wq': n(ks[6], (H, H), jnp.float32) * SCALE, 'Wo': n(ks[7], (H, 2 * H), jnp.float32) * SCALE, 'bo': jnp.zeros((H,), jnp.float32)}
    _L0_xattn_all = _L0_xattn_setup()
    _L0_xattn_in = {k: v for k, v in _L0_xattn_all.items() if k in ('Wi0', 'Wh0', 'bi0', 'bh0', 'Wi1', 'Wh1', 'bi1', 'bh1', 'Wq', 'Wo', 'bo')}
    del _L0_xattn_all

    def _L0_ffn_setup():
        import jax, jax.numpy as jnp
        import numpy as np

        def _ste(w, w_q):
            return w + jax.lax.stop_gradient(w_q - w)

        def quantize_w8_per(w, axis):
            amax = jnp.clip(jnp.max(jnp.abs(w), axis=axis, keepdims=True), 1e-08, None)
            scale = 127.0 / amax
            w_q = jnp.clip(jnp.round(w * scale), -128.0, 127.0) / scale
            return _ste(w, w_q)

        def quantize_a16(x):
            amax = jnp.clip(jnp.max(jnp.abs(x)), 1e-08, None)
            scale = 32767.0 / amax
            x_q = jnp.clip(jnp.round(x * scale), -32768.0, 32767.0) / scale
            return _ste(x, x_q)
        key = jax.random.key(seed)
        k1, k2, k3 = jax.random.split(key, 3)
        d_model, d_ff = (256, 1024)
        x = jax.random.normal(k1, (4, 512, d_model), dtype=jnp.float32)
        W_in = jax.random.normal(k2, (d_model, d_ff), dtype=jnp.float32) / np.sqrt(d_model)
        b_in = jnp.zeros((d_ff,), dtype=jnp.float32)
        W_out = jax.random.normal(k3, (d_ff, d_model), dtype=jnp.float32) / np.sqrt(d_ff)
        b_out = jnp.zeros((d_model,), dtype=jnp.float32)
        return {'x': x, 'W_in': W_in, 'b_in': b_in, 'W_out': W_out, 'b_out': b_out}
    _L0_ffn_all = _L0_ffn_setup()
    _L0_ffn_in = {k: v for k, v in _L0_ffn_all.items() if k in ('W_in', 'b_in', 'W_out', 'b_out')}
    del _L0_ffn_all

    def _L1_xattn_setup():
        import jax, jax.numpy as jnp
        import numpy as np
        NUM_HEADS = 16
        HIDDEN = 256
        B, S = (2, 512)

        def _split_heads(x, H):
            b, s, d = x.shape
            return x.reshape(b, s, H, d // H).transpose(0, 2, 1, 3)
        key = jax.random.key(seed)
        ks = jax.random.split(key, 14)
        D = HIDDEN
        scale = 1.0 / np.sqrt(D)
        inp = {'query': jax.random.normal(ks[0], (B, S, D), jnp.float32), 'key_in': jax.random.normal(ks[1], (B, S, D), jnp.float32), 'value': jax.random.normal(ks[2], (B, S, D), jnp.float32), 'group_prob': jax.random.uniform(ks[3], (B, S, S), jnp.float32), 'mask': jax.random.randint(ks[4], (B, S, S), 0, 2, jnp.int32), 'wq_k': jax.random.normal(ks[5], (D, D), jnp.float32) * scale, 'wq_b': jnp.zeros((D,), jnp.float32), 'wk_k': jax.random.normal(ks[6], (D, D), jnp.float32) * scale, 'wk_b': jnp.zeros((D,), jnp.float32), 'wv_k': jax.random.normal(ks[7], (D, D), jnp.float32) * scale, 'wv_b': jnp.zeros((D,), jnp.float32), 'wo_k': jax.random.normal(ks[8], (D, D), jnp.float32) * scale, 'wo_b': jnp.zeros((D,), jnp.float32)}
        return inp
    _L1_xattn_all = _L1_xattn_setup()
    _L1_xattn_in = {k: v for k, v in _L1_xattn_all.items() if k in ('wq_k', 'wq_b', 'wk_k', 'wk_b', 'wv_k', 'wv_b', 'wo_k', 'wo_b')}
    del _L1_xattn_all

    def _L1_ffn_setup():
        import jax, jax.numpy as jnp
        import numpy as np
        B, S, D = (4, 512, 256)
        E, F = (8, 1024)
        key = jax.random.key(seed)
        ks = jax.random.split(key, 5)
        x = jax.random.normal(ks[0], (B, S, D), dtype=jnp.float32)
        switch_w = jax.random.normal(ks[1], (D, E), dtype=jnp.float32) * D ** (-0.5)
        switch_b = jnp.zeros((E,), dtype=jnp.float32)
        w1 = jax.random.normal(ks[2], (E, D, F), dtype=jnp.float32) * D ** (-0.5)
        b1 = jnp.zeros((E, F), dtype=jnp.float32)
        w2 = jax.random.normal(ks[3], (E, F, D), dtype=jnp.float32) * F ** (-0.5)
        b2 = jnp.zeros((E, D), dtype=jnp.float32)
        return {'x': x, 'switch_w': switch_w, 'switch_b': switch_b, 'w1': w1, 'b1': b1, 'w2': w2, 'b2': b2}
    _L1_ffn_all = _L1_ffn_setup()
    _L1_ffn_in = {k: v for k, v in _L1_ffn_all.items() if k in ('switch_w', 'switch_b', 'w1', 'b1', 'w2', 'b2')}
    del _L1_ffn_all
    return {'x': x, 'ctx_1024': ctx_1024, 'fside_BxSxS2_0': fside_BxSxS2_0, 'mask_BxSxS2_ik1': mask_BxSxS2_ik1, 'L0_xattn_Wi0': _L0_xattn_in['Wi0'], 'L0_xattn_Wh0': _L0_xattn_in['Wh0'], 'L0_xattn_bi0': _L0_xattn_in['bi0'], 'L0_xattn_bh0': _L0_xattn_in['bh0'], 'L0_xattn_Wi1': _L0_xattn_in['Wi1'], 'L0_xattn_Wh1': _L0_xattn_in['Wh1'], 'L0_xattn_bi1': _L0_xattn_in['bi1'], 'L0_xattn_bh1': _L0_xattn_in['bh1'], 'L0_xattn_Wq': _L0_xattn_in['Wq'], 'L0_xattn_Wo': _L0_xattn_in['Wo'], 'L0_xattn_bo': _L0_xattn_in['bo'], 'L0_ffn_W_in': _L0_ffn_in['W_in'], 'L0_ffn_b_in': _L0_ffn_in['b_in'], 'L0_ffn_W_out': _L0_ffn_in['W_out'], 'L0_ffn_b_out': _L0_ffn_in['b_out'], 'L1_xattn_wq_k': _L1_xattn_in['wq_k'], 'L1_xattn_wq_b': _L1_xattn_in['wq_b'], 'L1_xattn_wk_k': _L1_xattn_in['wk_k'], 'L1_xattn_wk_b': _L1_xattn_in['wk_b'], 'L1_xattn_wv_k': _L1_xattn_in['wv_k'], 'L1_xattn_wv_b': _L1_xattn_in['wv_b'], 'L1_xattn_wo_k': _L1_xattn_in['wo_k'], 'L1_xattn_wo_b': _L1_xattn_in['wo_b'], 'L1_ffn_switch_w': _L1_ffn_in['switch_w'], 'L1_ffn_switch_b': _L1_ffn_in['switch_b'], 'L1_ffn_w1': _L1_ffn_in['w1'], 'L1_ffn_b1': _L1_ffn_in['b1'], 'L1_ffn_w2': _L1_ffn_in['w2'], 'L1_ffn_b2': _L1_ffn_in['b2']}

def reference(x, ctx_1024, fside_BxSxS2_0, mask_BxSxS2_ik1, L0_xattn_Wi0, L0_xattn_Wh0, L0_xattn_bi0, L0_xattn_bh0, L0_xattn_Wi1, L0_xattn_Wh1, L0_xattn_bi1, L0_xattn_bh1, L0_xattn_Wq, L0_xattn_Wo, L0_xattn_bo, L0_ffn_W_in, L0_ffn_b_in, L0_ffn_W_out, L0_ffn_b_out, L1_xattn_wq_k, L1_xattn_wq_b, L1_xattn_wk_k, L1_xattn_wk_b, L1_xattn_wv_k, L1_xattn_wv_b, L1_xattn_wo_k, L1_xattn_wo_b, L1_ffn_switch_w, L1_ffn_switch_b, L1_ffn_w1, L1_ffn_b1, L1_ffn_w2, L1_ffn_b2):
    import jax
    import jax.numpy as jnp

    def _L0_xattn_ref(inputs, context, Wi0, Wh0, bi0, bh0, Wi1, Wh1, bi1, bh1, Wq, Wo, bo):
        import jax, jax.numpy as jnp
        import numpy as np
        B, T, S, DIN, H = (64, 64, 64, 256, 256)
        SCALE = 0.02

        def _lstm_cell(x, h, c, Wi, Wh, bi, bh):
            g = x @ Wi.T + bi + h @ Wh.T + bh
            i, f, gg, o = jnp.split(g, 4, axis=-1)
            c2 = jax.nn.sigmoid(f) * c + jax.nn.sigmoid(i) * jnp.tanh(gg)
            h2 = jax.nn.sigmoid(o) * jnp.tanh(c2)
            return (h2, c2)
        b, t, _ = inputs.shape
        h = Wh0.shape[1]

        def step(carry, x_t):
            h0, c0, h1, c1, a = carry
            xin = jnp.concatenate([x_t, a], axis=-1)
            h0, c0 = _lstm_cell(xin, h0, c0, Wi0, Wh0, bi0, bh0)
            h1, c1 = _lstm_cell(h0, h1, c1, Wi1, Wh1, bi1, bh1)
            q = h1 @ Wq.T
            attn = jax.nn.softmax(jnp.einsum('bh,bsh->bs', q, context), axis=-1)
            mixed = jnp.einsum('bs,bsh->bh', attn, context)
            a2 = jnp.tanh(jnp.concatenate([mixed, h1], axis=-1) @ Wo.T + bo)
            return ((h0, c0, h1, c1, a2), a2)
        z = jnp.zeros((b, h), inputs.dtype)
        carry0 = (z, z, z, z, z)
        _, outs = jax.lax.scan(step, carry0, jnp.swapaxes(inputs, 0, 1))
        return jnp.swapaxes(outs, 0, 1)

    def _L0_ffn_ref(x, W_in, b_in, W_out, b_out):
        import jax, jax.numpy as jnp
        import numpy as np

        def _ste(w, w_q):
            return w + jax.lax.stop_gradient(w_q - w)

        def quantize_w8_per(w, axis):
            amax = jnp.clip(jnp.max(jnp.abs(w), axis=axis, keepdims=True), 1e-08, None)
            scale = 127.0 / amax
            w_q = jnp.clip(jnp.round(w * scale), -128.0, 127.0) / scale
            return _ste(w, w_q)

        def quantize_a16(x):
            amax = jnp.clip(jnp.max(jnp.abs(x)), 1e-08, None)
            scale = 32767.0 / amax
            x_q = jnp.clip(jnp.round(x * scale), -32768.0, 32767.0) / scale
            return _ste(x, x_q)
        W_in_sim = quantize_w8_per(W_in, axis=0)
        W_out_sim = quantize_w8_per(W_out, axis=1)
        x_sim = quantize_a16(x)
        hidden = jax.nn.gelu(x_sim @ W_in_sim + b_in, approximate=False)
        hidden_sim = quantize_a16(hidden)
        out = hidden_sim @ W_out_sim + b_out
        return out

    def _L1_xattn_ref(query, key_in, value, group_prob, mask, wq_k, wq_b, wk_k, wk_b, wv_k, wv_b, wo_k, wo_b):
        import jax, jax.numpy as jnp
        import numpy as np
        NUM_HEADS = 16
        HIDDEN = 256
        B, S = (2, 512)

        def _split_heads(x, H):
            b, s, d = x.shape
            return x.reshape(b, s, H, d // H).transpose(0, 2, 1, 3)
        H = NUM_HEADS
        dh = query.shape[-1] // H
        q = _split_heads(query @ wq_k + wq_b, H)
        k = _split_heads(key_in @ wk_k + wk_b, H)
        v = _split_heads(value @ wv_k + wv_b, H)
        logits = jnp.einsum('bhqd,bhkd->bhqk', q, k) / jnp.sqrt(jnp.asarray(dh, q.dtype))
        neg = (1.0 - mask.astype(q.dtype)) * -1000000000.0
        logits = logits + neg[:, None, :, :]
        attn = jax.nn.softmax(logits, axis=-1)
        attn = attn * group_prob[:, None, :, :]
        out = jnp.einsum('bhqk,bhkd->bhqd', attn, v)
        out = out.transpose(0, 2, 1, 3).reshape(query.shape[0], -1, H * dh)
        return out @ wo_k + wo_b

    def _L1_ffn_ref(x, switch_w, switch_b, w1, b1, w2, b2):
        import jax, jax.numpy as jnp
        import numpy as np
        B, S, D = (4, 512, 256)
        E, F = (8, 1024)
        b, s, d = x.shape
        t = x.reshape(-1, d)
        logits = t @ switch_w + switch_b
        route_prob = jax.nn.softmax(logits, axis=-1)
        route_prob_max = jnp.max(route_prob, axis=-1)
        routes = jnp.argmax(route_prob, axis=-1)
        out = jnp.zeros_like(t)
        n_experts = w1.shape[0]
        for e in range(n_experts):
            h = jax.nn.gelu(t @ w1[e] + b1[e])
            y = h @ w2[e] + b2[e]
            mask = (routes == e)[:, None]
            out = jnp.where(mask, y, out)
        out = out * route_prob_max[:, None]
        return out.reshape(b, s, d)
    x = x + _L0_xattn_ref(_layernorm(x, axis=-1), ctx_1024, L0_xattn_Wi0, L0_xattn_Wh0, L0_xattn_bi0, L0_xattn_bh0, L0_xattn_Wi1, L0_xattn_Wh1, L0_xattn_bi1, L0_xattn_bh1, L0_xattn_Wq, L0_xattn_Wo, L0_xattn_bo)
    x = x + _L0_ffn_ref(_layernorm(x, axis=-1), L0_ffn_W_in, L0_ffn_b_in, L0_ffn_W_out, L0_ffn_b_out)
    x = x + _L1_xattn_ref(_layernorm(x, axis=-1), ctx_1024, ctx_1024, fside_BxSxS2_0, mask_BxSxS2_ik1, L1_xattn_wq_k, L1_xattn_wq_b, L1_xattn_wk_k, L1_xattn_wk_b, L1_xattn_wv_k, L1_xattn_wv_b, L1_xattn_wo_k, L1_xattn_wo_b)
    x = x + _L1_ffn_ref(_layernorm(x, axis=-1), L1_ffn_switch_w, L1_ffn_switch_b, L1_ffn_w1, L1_ffn_b1, L1_ffn_w2, L1_ffn_b2)
    return x

_drawn_inputs = setup_inputs


def setup_inputs(seed=0):
    import zlib

    import numpy as np

    out = dict(_drawn_inputs(seed))
    spreads = {'L0_xattn_bi0': (0.0, 0.8),
     'L0_xattn_bh0': (0.0, 0.8),
     'L0_xattn_bi1': (0.0, 0.1),
     'L0_xattn_bh1': (0.0, 0.1),
     'L0_xattn_bo': (0.0, 0.1),
     'L0_ffn_b_in': (0.0, 0.1),
     'L0_ffn_b_out': (0.0, 0.1),
     'L1_xattn_wq_b': (0.0, 0.383),
     'L1_xattn_wk_b': (0.0, 0.8),
     'L1_xattn_wv_b': (0.0, 0.1),
     'L1_xattn_wo_b': (0.0, 0.1),
     'L1_ffn_switch_b': (0.0, 0.1),
     'L1_ffn_b1': (0.0, 0.384),
     'L1_ffn_b2': (0.0, 0.1)}
    factors = {'L0_xattn_Wi0': 6.318, 'L0_xattn_Wh0': 8.0, 'L0_xattn_Wi1': 4.561, 'L0_xattn_Wh1': 5.313}
    for name, (base, spread) in spreads.items():
        noise = np.random.default_rng([zlib.crc32(name.encode()), seed]).standard_normal(out[name].shape)
        drawn = base * np.exp(spread * noise) if base else spread * noise
        out[name] = jnp.asarray(drawn.astype(out[name].dtype))
    for name, factor in factors.items():
        out[name] = (out[name] * factor).astype(out[name].dtype)
    return out
```

```python
import numpy as np
import concourse.bass as bass
from concourse import mybir
from concourse.alu_op_type import AluOpType as ALU
from contextlib import ExitStack

F32 = mybir.dt.float32
BF16 = mybir.dt.bfloat16
I32 = mybir.dt.int32
ACT = mybir.ActivationFunctionType
AX = mybir.AxisListType

B, T, D, S = 4, 1024, 256, 64
FF = 1024
E = 8
H, DH = 16, 16
P = 128
NT = B * T // P
NB = T // P
KC = D // P
FC = FF // P
SLOT_TILES = 40
EPS = 1e-5
ROUND = 1.5 * 2.0 ** 23
GATES = 4
REDUCE_MAX = bass.bass_isa.ReduceOp.max


TAKEN = []


def release_semaphores(nc):
    with nc.Block() as block:
        @block.sync
        def _(sp):
            for taken in TAKEN:
                sp.sem_clear(taken)
    for taken in TAKEN:
        nc.release_semaphore(taken)
    TAKEN.clear()


class Pool:

    def __init__(self, nc, ctx, stage):
        self.nc, self.ctx, self.stage = nc, ctx, stage

    def sbuf(self, name, shape, dt=F32):
        return self.ctx.enter_context(self.nc.sbuf_tensor(f"{self.stage}_{name}", shape, dt))

    def psum(self, name, shape=(P, 512), dt=F32):
        return self.ctx.enter_context(self.nc.psum_tensor(f"{self.stage}_{name}", list(shape), dt))

    def sem(self, name):
        taken = self.nc.alloc_semaphore(f"{self.stage}_{name}")
        TAKEN.append(taken)
        return taken


def norm_memory(pool):
    m = {n: pool.sbuf(f"norm_{n}", [P, w]) for n, w in
         (("held", 1), ("stats", 6), ("mean_var", 2), ("std", 1), ("rstd", 1), ("eps", 1))}
    m.update({f"{n}_done": pool.sem(f"norm_{n}_done") for n in ("eps", "stats", "mean_var", "std", "rstd")})
    return m


def norm_vector(nc, dve, m, n, x, out):
    nc.vector.memset(m["held"][:], 0.0)
    nc.vector.bn_stats(m["stats"][:], x).then_inc(m["stats_done"], 1)
    dve.wait_ge(m["stats_done"], n)
    nc.vector.memset(m["held"][:], 0.0)
    nc.vector.bn_aggr(m["mean_var"][:], m["stats"][:]).then_inc(m["mean_var_done"], 1)
    dve.wait_ge(m["std_done"], n)
    nc.vector.reciprocal(m["rstd"][:], m["std"][:]).then_inc(m["rstd_done"], 1)
    dve.wait_ge(m["rstd_done"], n)
    return nc.vector.tensor_scalar(out, x, m["mean_var"][:, 0:1], m["rstd"][:], ALU.subtract, ALU.mult)


def norm_scalar(nc, act, m, n):
    act.wait_ge(m["mean_var_done"], n)
    nc.scalar.activation(m["std"][:], m["mean_var"][:, 1:2], ACT.Sqrt, bias=m["eps"][:]).then_inc(m["std_done"], 1)


def halve_sigmoid_gates(nc, tile, low, last_sem):
    nc.vector.tensor_scalar(tile[:, :, 0:3, :], tile[:, :, 0:3, :], 0.5 * low, None, ALU.mult).then_inc(last_sem, 1)
    if low != 1.0:
        nc.vector.tensor_scalar(tile[:, :, 3, :], tile[:, :, 3, :], low, None, ALU.mult).then_inc(last_sem, 1)


def make_identity(nc, pool_engine, ident, zeroed, done):
    nc.gpsimd.memset(ident[:], 0.0).then_inc(zeroed, 1)
    pool_engine.wait_ge(zeroed, 1)
    nc.gpsimd.affine_select(out=ident[:], in_=ident[:], compare_op=ALU.not_equal, fill=1.0, base=0,
                            pattern=[[-1, P]], channel_multiplier=1).then_inc(done, 1)


def prepare_scan(nc, ins, w):
    with ExitStack() as ctx:
        m = Pool(nc, ctx, "prep")
        wq = m.sbuf("wq", [P, KC, 2, P])
        womt = m.sbuf("womt", [P, KC, D])
        ctx_split = m.sbuf("ctx_split", [P, KC, 2, P])
        bias = [m.sbuf(f"bias{i}", [P, GATES, 64]) for i in range(2)]
        wx_bias2 = m.sbuf("wx_bias2", [P, 4, GATES, 64])
        kp = [m.psum(f"kp{k}") for k in range(2)]
        vp = [m.psum(f"vp{k}") for k in range(2)]
        zeroed, ident_done, rows_zeroed = m.sem("zeroed"), m.sem("ident_done"), m.sem("rows_zeroed")
        fold_in, scan_in, bias_in = m.sem("fold_in"), m.sem("scan_in"), m.sem("bias_in")
        folded, scaled = m.sem("folded"), m.sem("scaled")
        with nc.Block() as block:
            @block.sync
            def _(sp):
                for dst, src in ((wq, "wq"), (w["ctxT"], "ctxT"), (womt, "wo_mixed"), (ctx_split, "ctx_split")):
                    sp.dma_start(dst[:], ins[src]).then_inc(fold_in, 16)
                for name in ("wx", "wa", "wh0", "wi1", "wh1", "woh"):
                    sp.dma_start(w[name][:], ins[name]).then_inc(scan_in, 16)
                sp.dma_start(w["wx_bias"][:], ins["bi0"].partition_broadcast(P)).then_inc(bias_in, 16)
                sp.dma_start(wx_bias2[:], ins["bh0"].partition_broadcast(P)).then_inc(bias_in, 16)
                sp.wait_ge(rows_zeroed, 3)
                for j in range(4):
                    rows = slice(32 * j, 32 * j + B)
                    sp.dma_start(bias[0][rows], ins["bi1"][j].partition_broadcast(B)).then_inc(bias_in, 16)
                    sp.dma_start(bias[1][rows], ins["bh1"][j].partition_broadcast(B)).then_inc(bias_in, 16)
                    sp.dma_start(w["bo"][rows], ins["bo"][j].partition_broadcast(B)).then_inc(bias_in, 16)

            @block.gpsimd
            def _(pool):
                for tile in (bias[0], bias[1]):
                    nc.gpsimd.memset(tile[:].rearrange("p g u -> p (g u)"), 0.0).then_inc(rows_zeroed, 1)
                nc.gpsimd.memset(w["bo"][:], 0.0).then_inc(rows_zeroed, 1)
                make_identity(nc, pool, w["ident"], zeroed, ident_done)
                nc.gpsimd.memset(w["off_rows"][:], 1e30).then_inc(zeroed, 1)
                for j in range(4):
                    pool.wait_ge(zeroed, 2 + j)
                    nc.gpsimd.affine_select(out=w["off_rows"][:], in_=w["off_rows"][:], compare_op=ALU.not_equal,
                                            fill=-1e30, base=-33 * j, pattern=[[0, 1]],
                                            channel_multiplier=1).then_inc(zeroed, 1)
                pool.wait_ge(zeroed, 6)
                pool.wait_ge(ident_done, 1)

            @block.tensor
            def _(pe):
                pe.wait_ge(fold_in, 64)
                for k in range(2):
                    for c in range(KC):
                        nc.tensor.matmul(kp[k][:, 0:B * S], wq[:, c, k, :], w["ctxT"][:, c, :],
                                         start=c == 0, stop=c == KC - 1)
                    for c in range(KC):
                        last = nc.tensor.matmul(vp[k][:, 0:D], ctx_split[:, c, k, :], womt[:, c, :],
                                                start=c == 0, stop=c == KC - 1)
                last.then_inc(folded, 1)

            @block.vector
            def _(dve):
                dve.wait_ge(bias_in, 16 * (2 + 12))
                nc.vector.tensor_tensor(w["wx_bias"][:], w["wx_bias"][:], wx_bias2[:], ALU.add).then_inc(scaled, 1)
                nc.vector.tensor_tensor(w["b1"][:], bias[0][:], bias[1][:], ALU.add).then_inc(scaled, 1)
                dve.wait_ge(scaled, 2)
                halve_sigmoid_gates(nc, w["wx_bias"], 1.0, scaled)
                nc.vector.tensor_scalar(w["b1"][:, 0:3, :], w["b1"][:, 0:3, :], 0.5, None, ALU.mult).then_inc(scaled, 1)
                dve.wait_ge(scan_in, 6 * 16)
                gated = "p k (j g u) -> p (k j) g u"
                halve_sigmoid_gates(nc, w["wx"][:].rearrange(gated, j=4, g=GATES), 1.0, scaled)
                for name, low in (("wa", 1.0), ("wh0", 0.5), ("wi1", 0.5), ("wh1", 0.5)):
                    halve_sigmoid_gates(nc, w[name][:].rearrange("p k j (g u) -> p (k j) g u", g=GATES), low, scaled)
                nc.vector.tensor_scalar(w["woh"][:], w["woh"][:], 0.5, None, ALU.mult).then_inc(scaled, 1)
                dve.wait_ge(folded, 1)
                for k in range(2):
                    nc.vector.tensor_scalar(w["kp"][:, k, :, :].rearrange("p b s -> p (b s)"), kp[k][:, 0:B * S], 0.5,
                                            None, ALU.mult).then_inc(scaled, 1)
                    nc.vector.tensor_copy(w["vp"][:, k, :, :].rearrange("p j u -> p (j u)"),
                                          vp[k][:, 0:D]).then_inc(scaled, 1)
                dve.wait_ge(scaled, 17)


def input_gates(nc, x_steps, gx_scratch, w):
    with ExitStack() as ctx:
        m = Pool(nc, ctx, "gx")
        norm = norm_memory(m)
        x = [m.sbuf(f"x{i}", [P, D]) for i in range(2)]
        xn = [m.sbuf(f"xn{i}", [P, D]) for i in range(2)]
        xT = [m.sbuf(f"xT{i}", [P, KC, P]) for i in range(2)]
        out = [m.sbuf(f"out{i}", [P, 4 * D]) for i in range(2)]
        turned = [m.psum(f"turned{i}") for i in range(2)]
        summed = [[m.psum(f"summed{i}_{n}") for n in range(2)] for i in range(2)]
        x_in = [m.sem(f"x_in{i}") for i in range(2)]
        stored = [m.sem(f"stored{i}") for i in range(2)]
        xn_done, turned_done, xT_done, sum_done, out_done = (
            m.sem(n) for n in ("xn_done", "turned_done", "xT_done", "sum_done", "out_done"))
        with nc.Block() as block:
            @block.sync
            def _(sp):
                for s in range(2):
                    sp.dma_start(x[s][:], x_steps[P * s:P * s + P, :]).then_inc(x_in[s], 16)
                with sp.Fori(0, NT // 2 - 1) as i:
                    for s in range(2):
                        sp.wait_ge(out_done, 2 * i + s + 1)
                        sp.dma_start(gx_scratch[bass.ds(i * 2 * P + P * s, P), :], out[s][:]).then_inc(stored[s], 16)
                        sp.dma_start(x[s][:], x_steps[bass.ds(i * 2 * P + P * (s + 2), P), :]).then_inc(x_in[s], 16)
                for s in range(2):
                    sp.wait_ge(out_done, NT - 1 + s)
                    sp.dma_start(gx_scratch[P * (NT - 2 + s):P * (NT - 1 + s), :], out[s][:]).then_inc(stored[s], 16)
                for s in range(2):
                    sp.wait_ge(stored[s], 8 * NT)

            @block.tensor
            def _(pe):
                with pe.Fori(0, NT // 2) as i:
                    for s in range(2):
                        n = 2 * i + s + 1
                        pe.wait_ge(xn_done, n)
                        for c in range(KC):
                            last = nc.tensor.transpose(turned[s][:, P * c:P * c + P], xn[s][:, P * c:P * c + P], w["ident"][:])
                        last.then_inc(turned_done, 1)
                        pe.wait_ge(xT_done, n)
                        for h in range(2):
                            for c in range(KC):
                                last = nc.tensor.matmul(summed[s][h][:], xT[s][:, c, :], w["wx"][:, c, 512 * h:512 * h + 512],
                                                        start=c == 0, stop=c == KC - 1)
                        last.then_inc(sum_done, 1)

            @block.scalar
            def _(act):
                act.wait_ge(norm["eps_done"], 1)
                with act.Fori(0, NT // 2) as i:
                    for s in range(2):
                        n = 2 * i + s + 1
                        norm_scalar(nc, act, norm, n)
                        act.wait_ge(turned_done, n)
                        nc.scalar.activation(xT[s][:].rearrange("p c n -> p (c n)"), turned[s][:, 0:D], ACT.Copy).then_inc(xT_done, 1)

            @block.vector
            def _(dve):
                nc.vector.memset(norm["eps"][:], EPS).then_inc(norm["eps_done"], 1)
                bias = w["wx_bias"][:].rearrange("p j g u -> p (j g u)")
                def normalize(n, s, seen):
                    dve.wait_ge(x_in[s], seen)
                    norm_vector(nc, dve, norm, n, x[s][:], xn[s][:]).then_inc(xn_done, 1)
                def evacuate(n, s):
                    dve.wait_ge(sum_done, n)
                    for h in range(2):
                        last = nc.vector.tensor_tensor(out[s][:, 512 * h:512 * h + 512], summed[s][h][:],
                                                       bias[:, 512 * h:512 * h + 512], ALU.add)
                    last.then_inc(out_done, 1)
                normalize(1, 0, 16)
                normalize(2, 1, 16)
                evacuate(1, 0)
                normalize(3, 0, 32)
                evacuate(2, 1)
                with dve.Fori(1, NT // 2 - 1) as i:
                    for s in range(2):
                        n = 2 * i + s + 1
                        normalize(n + 1, 1 - s, 16 * i + 16 + 16 * s)
                        dve.wait_ge(stored[s], 16 * i)
                        evacuate(n, s)
                normalize(NT, 1, 8 * NT)
                dve.wait_ge(stored[0], 8 * NT - 16)
                evacuate(NT - 1, 0)
                dve.wait_ge(stored[1], 8 * NT - 16)
                evacuate(NT, 1)


def scan(nc, gx_scratch, a_hist, w):
    U = 8
    HALF = U // 2
    LOADED = 16 * 4
    with ExitStack() as ctx:
        m = Pool(nc, ctx, "scan")
        gx = [m.sbuf(f"gx{i}", [P, HALF, GATES * 64]) for i in range(2)]
        cell = [m.sbuf(f"cell{l}", [P, GATES + 1, 2, B]) for l in range(2)]
        uv = [m.sbuf(f"uv{l}", [P, 2, 2, B]) for l in range(2)]
        tanh_c = [m.sbuf(f"tanh_c{l}", [P, 2, B]) for l in range(2)]
        hT = [m.sbuf(f"hT{l}", [P, 2, B]) for l in range(2)]
        aT = m.sbuf("aT", [P, 2, B])
        probs, normed, pT = m.sbuf("probs", [P, S + 1]), m.sbuf("normed", [P, S]), m.sbuf("pT", [P, 2, 32])
        neg_max, inv = m.sbuf("neg_max", [P, 1]), m.sbuf("inv", [P, 1])
        sums = [m.psum("gates0"), m.psum("gates1")]
        scores, a_sum = m.psum("scores"), m.psum("a_sum")
        turned = [m.psum(f"turned{l}") for l in range(2)]
        gatesT = [turned[l][:, 0:256].rearrange("p (g k u) -> p g k u", g=GATES, k=2) for l in range(2)]
        a_sumT = turned[0][:, 256:320]
        total = turned[1][:, 256:257]
        gates_summed = [m.sem(f"gates_summed{l}") for l in range(2)]
        gates_turned = [m.sem(f"gates_turned{l}") for l in range(2)]
        gates_tanh = [m.sem(f"gates_tanh{l}") for l in range(2)]
        uv_done = [m.sem(f"uv_done{l}") for l in range(2)]
        c_done = [m.sem(f"c_done{l}") for l in range(2)]
        tanh_c_done = [m.sem(f"tanh_c_done{l}") for l in range(2)]
        h_ready = [m.sem(f"h_ready{l}") for l in range(2)]
        a_ready = m.sem("a_ready")
        scores_done, max_done, probs_done, inv_done, probs_normed, probs_turned, a_summed, a_turned, a_kept, zeroed = (
            m.sem(n) for n in ("scores_done", "max_done", "probs_done", "inv_done", "probs_normed", "probs_turned",
                               "a_summed", "a_turned", "a_kept", "zeroed"))
        gx_loaded = [m.sem(f"gx_loaded{i}") for i in range(2)]
        with nc.Block() as block:
            @block.sync
            def _(sp):
                def load(half, t):
                    for j in range(4):
                        sp.dma_start(gx[half][32 * j:32 * j + B, :, :],
                                     gx_scratch[bass.ds(t, HALF), :, j, :].rearrange("t b n -> b t n")).then_inc(gx_loaded[half], 16)
                sp.wait_ge(zeroed, 1)
                load(0, 0)
                load(1, HALF)
                with sp.Fori(0, T // U - 1) as i:
                    t = i * U
                    sp.wait_ge(scores_done, t + HALF)
                    load(0, t + U)
                    sp.wait_ge(scores_done, t + U)
                    load(1, t + U + HALF)

            @block.tensor
            def _(pe):
                def product(bank, state, weight, n, start, stop):
                    for k in range(2):
                        for j in range(4):
                            last = nc.tensor.matmul(bank[32 * j:32 * j + B, 0:n], state[:, k, 0:B], weight[:, k, j, :],
                                                    start=start and k == 0, stop=stop and k == 1, skip_group_check=True)
                    return last

                def seed(bank, rows, n):
                    nc.tensor.matmul(bank[:, 0:n], w["ident"][:], rows, start=True, stop=False, skip_group_check=True)
                bias1 = w["b1"][:].rearrange("p g u -> p (g u)")

                def step(t, s, loaded=None, last=False):
                    pe.wait_ge(a_ready, t + s + 1)
                    product(sums[0], aT, w["wa"], 256, False, True).then_inc(gates_summed[0], 1)
                    product(sums[1], hT[1], w["wh1"], 256, False, False)
                    pe.wait_ge(h_ready[0], t + s + 2)
                    product(sums[1], hT[0], w["wi1"], 256, False, True).then_inc(gates_summed[1], 1)
                    if not last:
                        if loaded is not None:
                            pe.wait_ge(gx_loaded[(s + 1) // HALF % 2], loaded)
                        seed(sums[0], gx[(s + 1) // HALF % 2][:, (s + 1) % HALF, :], 256)
                        product(sums[0], hT[0], w["wh0"], 256, False, False)
                    pe.wait_ge(h_ready[1], t + s + 2)
                    product(scores, hT[1], w["kp"], S, True, True).then_inc(scores_done, 1)
                    seed(a_sum, w["bo"][:], 64)
                    product(a_sum, hT[1], w["woh"], 64, False, False)
                    if not last:
                        seed(sums[1], bias1, 256)
                    pe.wait_ge(probs_turned, t + s + 1)
                    product(a_sum, pT, w["vp"], 64, False, True).then_inc(a_summed, 1)
                pe.wait_ge(zeroed, 1)
                pe.wait_ge(gx_loaded[0], LOADED)
                seed(sums[0], gx[0][:, 0, :], 256)
                seed(sums[1], bias1, 256)
                per_step = LOADED // U
                with pe.Fori(0, T // U - 1) as i:
                    t = i * U
                    for s in range(U):
                        step(t, s, {HALF - 1: t * per_step + LOADED, U - 1: t * per_step + 2 * LOADED}.get(s))
                for s in range(U):
                    step(T - U, s, T * per_step if s == HALF - 1 else None, last=s == U - 1)

            @block.scalar
            def _(act):
                def step(t, s):
                    n = t + s + 1
                    for l in range(2):
                        act.wait_ge(gates_turned[l], n)
                        nc.scalar.activation(cell[l][:, 0:GATES, :, :], gatesT[l][:, :, :, 0:B], ACT.Tanh).then_inc(gates_tanh[l], 1)
                        act.wait_ge(c_done[l], n)
                        nc.scalar.activation(tanh_c[l][:], cell[l][:, GATES, :, :], ACT.Tanh, scale=0.5).then_inc(tanh_c_done[l], 1)
                    act.wait_ge(max_done, n)
                    nc.scalar.activation(probs[:], scores[:, 0:S + 1], ACT.Exp, bias=neg_max[:], accum_out=total).then_inc(probs_done, 1)
                    act.wait_ge(a_turned, n)
                    nc.scalar.activation(aT[:], a_sumT.rearrange("p (k u) -> p k u", k=2)[:, :, 0:B], ACT.Tanh).then_inc(a_ready, 1)
                with act.Fori(0, T // U) as i:
                    for s in range(U):
                        step(i * U, s)

            @block.vector
            def _(dve):
                for tile in gx:
                    nc.vector.memset(tile[:], 0.0)
                for l in range(2):
                    nc.vector.memset(cell[l][:, GATES, :, :], 0.0)
                    nc.vector.memset(hT[l][:], 0.0).then_inc(h_ready[l], 1)
                nc.vector.memset(scores[:, 0:S], 0.0)
                nc.vector.tensor_copy(scores[:, S:S + 1], w["off_rows"][:])
                nc.vector.memset(aT[:], 0.0).then_inc(a_ready, 1)
                dve.wait_ge(a_ready, 1)
                nc.vector.memset(pT[:], 0.0).then_inc(zeroed, 1)

                def step(t, s):
                    n = t + s + 1
                    for l in range(2):
                        dve.wait_ge(gates_summed[l], n)
                        nc.vector.transpose(turned[l][:, 0:256], sums[l][:, 0:256]).then_inc(gates_turned[l], 1)
                        dve.wait_ge(gates_tanh[l], n)
                        nc.vector.scalar_tensor_tensor(uv[l][:], cell[l][:, 1:3, :, :], 1.0, cell[l][:, 3:5, :, :],
                                                       ALU.add, ALU.mult).then_inc(uv_done[l], 1)
                        dve.wait_ge(uv_done[l], n)
                        nc.vector.scalar_tensor_tensor(cell[l][:, GATES, :, :], uv[l][:, 1, :, :], 0.5, uv[l][:, 0, :, :],
                                                       ALU.mult, ALU.add).then_inc(c_done[l], 1)
                        dve.wait_ge(tanh_c_done[l], n)
                        nc.vector.scalar_tensor_tensor(hT[l][:], cell[l][:, 0, :, :], 1.0, tanh_c[l][:],
                                                       ALU.add, ALU.mult).then_inc(h_ready[l], 1)
                    dve.wait_ge(scores_done, n)
                    nc.vector.tensor_reduce(neg_max[:], scores[:, 0:S + 1], AX.X, ALU.max, negate=True).then_inc(max_done, 1)
                    dve.wait_ge(probs_done, n)
                    nc.vector.reciprocal(inv[:], total).then_inc(inv_done, 1)
                    dve.wait_ge(inv_done, n)
                    nc.vector.tensor_scalar(normed[:], probs[:, 0:S], inv[:], None, ALU.mult).then_inc(probs_normed, 1)
                    dve.wait_ge(probs_normed, n)
                    nc.vector.transpose(pT[:].rearrange("p k s -> p (k s)"), normed[:]).then_inc(probs_turned, 1)
                    dve.wait_ge(a_summed, n)
                    nc.vector.transpose(a_sumT, a_sum[:, 0:64]).then_inc(a_turned, 1)
                    dve.wait_ge(a_ready, n + 1)
                    nc.vector.tensor_scalar(a_hist[:, bass.ds(t + s, 1), :, :].rearrange("p t k b -> p (t k b)"),
                                            aT[:].rearrange("p k b -> p (k b)"), 1.0, None, ALU.mult).then_inc(a_kept, 1)
                with dve.Fori(0, T // U) as i:
                    for s in range(U):
                        step(i * U, s)
                dve.wait_ge(a_kept, T)


def quantize_rows(nc, stage, src, weight, back, scaled_back):
    with ExitStack() as ctx:
        m = Pool(nc, ctx, stage)
        amax, scale = m.sbuf("amax", [P, FC]), m.sbuf("scale", [P, FC])
        loaded, step = m.sem("loaded"), m.sem("step")
        with nc.Block() as block:
            @block.sync
            def _(sp):
                sp.dma_start(weight, src).then_inc(loaded, 16)

            @block.vector
            def _(dve):
                dve.wait_ge(loaded, 16)
                nc.vector.tensor_reduce(amax[:], weight, AX.X, ALU.max, apply_absolute_value=True).then_inc(step, 1)
                dve.wait_ge(step, 1)
                nc.vector.tensor_scalar(amax[:], amax[:], 1e-8, None, ALU.max).then_inc(step, 1)
                dve.wait_ge(step, 2)
                nc.vector.reciprocal(scale[:], amax[:]).then_inc(step, 1)
                nc.vector.tensor_scalar(back, amax[:], 1.0 / 127.0, None, ALU.mult).then_inc(step, 1)
                dve.wait_ge(step, 4)
                nc.vector.tensor_scalar(scale[:], scale[:], 127.0, None, ALU.mult).then_inc(step, 1)
                dve.wait_ge(step, 5)
                for f in range(FC):
                    nc.vector.tensor_scalar(weight[:, f, :], weight[:, f, :], scale[:, f:f + 1], 127.0,
                                            ALU.mult, ALU.min).then_inc(step, 1)
                dve.wait_ge(step, 5 + FC)
                nc.vector.tensor_scalar(weight, weight, ROUND, ROUND, ALU.add, ALU.subtract).then_inc(step, 1)
                dve.wait_ge(step, 6 + FC)
                if scaled_back:
                    for f in range(FC):
                        nc.vector.tensor_scalar(weight[:, f, :], weight[:, f, :], back[:, f:f + 1], None,
                                                ALU.mult).then_inc(step, 1)
                    dve.wait_ge(step, 6 + 2 * FC)


def turn_first_weight(nc, ins, raw, w):
    with ExitStack() as ctx:
        m = Pool(nc, ctx, "turn")
        turned = [m.psum(f"turned{i}") for i in range(2)]
        loaded, turned_done, copied = m.sem("loaded"), m.sem("turned_done"), m.sem("copied")
        with nc.Block() as block:
            @block.sync
            def _(sp):
                sp.dma_start(w["b_in"][:], ins["b_in"]).then_inc(loaded, 16)
                sp.wait_ge(loaded, 16)

            @block.tensor
            def _(pe):
                for f in range(FC):
                    if f >= 2:
                        pe.wait_ge(copied, f - 1)
                    for c in range(KC):
                        last = nc.tensor.transpose(turned[f % 2][:, P * c:P * c + P], raw[:, f, P * c:P * c + P],
                                                   w["ident"][:])
                    last.then_inc(turned_done, 1)

            @block.scalar
            def _(act):
                for f in range(FC):
                    act.wait_ge(turned_done, f + 1)
                    nc.scalar.activation(w["w_in"][:, :, P * f:P * f + P],
                                         turned[f % 2][:, 0:D].rearrange("p (c n) -> p c n", c=KC),
                                         ACT.Copy).then_inc(copied, 1)
                act.wait_ge(copied, FC)


def add_attention_and_normalize(nc, x_tokens, a_hist, xres, xn, norm_max, w):
    with ExitStack() as ctx:
        m = Pool(nc, ctx, "first")
        norm = norm_memory(m)
        part = [m.sbuf(f"part{i}", [P, KC, P]) for i in range(2)]
        row_max = m.sbuf("row_max", [P, NB, B])
        amax = m.sbuf("amax", [P, 1])
        turned = [m.psum(f"turned{i}") for i in range(2)]
        loaded, part_done, turned_done, sum_done, xn_done, row_max_done, max_done, all_done = (m.sem(n) for n in (
            "loaded", "part_done", "turned_done", "sum_done", "xn_done", "row_max_done", "max_done", "all_done"))
        with nc.Block() as block:
            @block.sync
            def _(sp):
                for b in range(B):
                    sp.dma_start(xres[:, :, b, :], x_tokens[b].rearrange("(g p) d -> p g d", p=P)).then_inc(loaded, 16)

            @block.gpsimd
            def _(pool):
                nc.gpsimd.sem_inc(turned_done, 2)
                with pool.Fori(0, NB) as g:
                    for b in range(B):
                        pool.wait_ge(turned_done, B * g + b + 1)
                        for k in range(2):
                            last = nc.gpsimd.tensor_copy(part[b % 2][:, k, :], a_hist[:, bass.ds(g * P, P), k, b])
                        last.then_inc(part_done, 1)
                pool.wait_ge(max_done, 1)
                nc.gpsimd.partition_all_reduce(norm_max[:], amax[:], P, REDUCE_MAX).then_inc(all_done, 1)
                pool.wait_ge(all_done, 1)

            @block.tensor
            def _(pe):
                nc.tensor.sem_inc(sum_done, 2)
                with pe.Fori(0, NB) as g:
                    for b in range(B):
                        pe.wait_ge(part_done, B * g + b + 1)
                        pe.wait_ge(sum_done, B * g + b + 1)
                        for k in range(2):
                            last = nc.tensor.transpose(turned[b % 2][:, P * k:P * k + P], part[b % 2][:, k, :], w["ident"][:])
                        last.then_inc(turned_done, 1)

            @block.scalar
            def _(act):
                act.wait_ge(norm["eps_done"], 1)
                with act.Fori(0, NB) as g:
                    for b in range(B):
                        norm_scalar(nc, act, norm, B * g + b + 1)

            @block.vector
            def _(dve):
                nc.vector.memset(norm["eps"][:], EPS).then_inc(norm["eps_done"], 1)
                dve.wait_ge(loaded, 16 * B)
                with dve.Fori(0, NB) as g:
                    for b in range(B):
                        n = B * g + b + 1
                        x = xres[:, bass.ds(g, 1), b, :].rearrange("p g d -> p (g d)")
                        normed = xn[:, bass.ds(g, 1), b, :].rearrange("p g d -> p (g d)")
                        dve.wait_ge(turned_done, n + 2)
                        for k in range(2):
                            half = x.rearrange("p (j k r) -> p j k r", j=4, k=2)[:, :, k, :]
                            last = nc.vector.tensor_tensor(half, turned[b % 2][:, P * k:P * k + P].rearrange("p (j r) -> p j r", j=4),
                                                           half, ALU.add)
                        last.then_inc(sum_done, 1)
                        dve.wait_ge(sum_done, n + 2)
                        norm_vector(nc, dve, norm, n, x, normed).then_inc(xn_done, 1)
                        dve.wait_ge(xn_done, n)
                        nc.vector.tensor_reduce(row_max[:, bass.ds(g, 1), b], normed, AX.X, ALU.max,
                                                apply_absolute_value=True).then_inc(row_max_done, 1)
                dve.wait_ge(row_max_done, NT)
                nc.vector.tensor_reduce(amax[:], row_max[:], AX.XY, ALU.max).then_inc(max_done, 1)


def range_scale(nc, dve, largest, scale, back, step, top):
    nc.vector.tensor_scalar(largest[:], largest[:], 1e-8, None, ALU.max).then_inc(step, 1)
    dve.wait_ge(step, 1)
    nc.vector.reciprocal(scale[:], largest[:]).then_inc(step, 1)
    dve.wait_ge(step, 2)
    nc.vector.tensor_scalar(scale[:], scale[:], top, None, ALU.mult).then_inc(step, 1)
    nc.vector.tensor_scalar(back[:], largest[:], 1.0 / top, None, ALU.mult).then_inc(step, 1)
    dve.wait_ge(step, 4)


def ffn_hidden(nc, xn, norm_max, hidden, hidden_max, w):
    with ExitStack() as ctx:
        m = Pool(nc, ctx, "hidden")
        scale, back = m.sbuf("scale", [P, 1]), m.sbuf("back", [P, 1])
        back_in = m.sbuf("back_in", [P, FC])
        xq = [m.sbuf(f"xq{i}", [P, D]) for i in range(2)]
        parts = m.sbuf("parts", [P, 2, KC, 4 * P], BF16)
        row_max = m.sbuf("row_max", [P, NB, FC])
        amax = m.sbuf("amax", [P, 1])
        turned = [m.psum(f"turned{i}") for i in range(2)]
        summed = [m.psum(f"summed{i}") for i in range(4)]
        step, scaled_done, xq_done, turned_done, high_done, low_done, sum_done, gelu_done, row_max_done, max_done, all_done = (
            m.sem(n) for n in ("step", "scaled_done", "xq_done", "turned_done", "high_done", "low_done", "sum_done",
                               "gelu_done", "row_max_done", "max_done", "all_done"))
        with nc.Block() as block:
            @block.gpsimd
            def _(pool):
                pool.wait_ge(max_done, 1)
                nc.gpsimd.partition_all_reduce(hidden_max[:], amax[:], P, REDUCE_MAX).then_inc(all_done, 1)
                pool.wait_ge(all_done, 1)

            @block.tensor
            def _(pe):
                nc.tensor.sem_inc(low_done, 2)
                nc.tensor.sem_inc(gelu_done, 4)

                def turn(g, b):
                    pe.wait_ge(xq_done, B * g + b + 1)
                    pe.wait_ge(low_done, B * g + b + 1)
                    for c in range(KC):
                        last = nc.tensor.transpose(turned[b % 2][:, P * c:P * c + P], xq[b % 2][:, P * c:P * c + P], w["ident"][:])
                    last.then_inc(turned_done, 1)

                def products(g):
                    for f in range(FC):
                        if f == 0:
                            pe.wait_ge(low_done, B * g + B + 2)
                        pe.wait_ge(gelu_done, FC * g + f + 1)
                        for part in range(2):
                            for c in range(KC):
                                last = nc.tensor.matmul(summed[f % 4][:], w["w_in"][:, c, P * f:P * f + P], parts[:, part, c, :],
                                                        start=part == 0 and c == 0, stop=part == 1 and c == KC - 1)
                        last.then_inc(sum_done, 1)
                with pe.Fori(0, NB) as g:
                    for b in range(B):
                        turn(g, b)
                    products(g)

            @block.scalar
            def _(act):
                act.wait_ge(step, 5)

                def split(g):
                    for b in range(B):
                        act.wait_ge(turned_done, B * g + b + 1)
                        nc.scalar.activation(parts[:, 0, :, P * b:P * b + P],
                                             turned[b % 2][:, 0:D].rearrange("p (c n) -> p c n", c=KC), ACT.Copy).then_inc(high_done, 1)

                def gelus(g):
                    for f in range(FC):
                        act.wait_ge(sum_done, FC * g + f + 1)
                        nc.scalar.activation(hidden[:, f, bass.ds(g * 4 * P, 4 * P)], summed[f % 4][:], ACT.Gelu,
                                             bias=w["b_in"][:, f:f + 1], scale=back_in[:, f:f + 1]).then_inc(gelu_done, 1)
                with act.Fori(0, NB) as g:
                    split(g)
                    gelus(g)

            @block.vector
            def _(dve):
                range_scale(nc, dve, norm_max, scale, back, step, 32767.0)
                nc.vector.tensor_scalar(back_in[:], w["back"][:], back[:], None, ALU.mult).then_inc(step, 1)

                def quantize(g, b):
                    n = B * g + b + 1
                    nc.vector.tensor_scalar(xq[b % 2][:], xn[:, bass.ds(g, 1), b, :].rearrange("p g d -> p (g d)"), scale[:], 32767.0,
                                            ALU.mult, ALU.min).then_inc(scaled_done, 1)
                    dve.wait_ge(scaled_done, n)
                    nc.vector.tensor_scalar(xq[b % 2][:], xq[b % 2][:], ROUND, ROUND, ALU.add, ALU.subtract).then_inc(xq_done, 1)

                def low(g, b):
                    n = B * g + b + 1
                    dve.wait_ge(high_done, n)
                    nc.vector.tensor_tensor(parts[:, 1, :, P * b:P * b + P],
                                            turned[b % 2][:, 0:D].rearrange("p (c n) -> p c n", c=KC),
                                            parts[:, 0, :, P * b:P * b + P], ALU.subtract).then_inc(low_done, 1)

                def largest(g):
                    for f in range(FC):
                        dve.wait_ge(gelu_done, FC * g + f + 5)
                        nc.vector.tensor_reduce(row_max[:, bass.ds(g, 1), f], hidden[:, f, bass.ds(g * 4 * P, 4 * P)],
                                                AX.X, ALU.max, apply_absolute_value=True).then_inc(row_max_done, 1)
                with dve.Fori(0, NB) as g:
                    quantize(g, 0)
                    quantize(g, 1)
                    for b in range(B):
                        low(g, b)
                        if b + 2 < B:
                            quantize(g, b + 2)
                    largest(g)
                dve.wait_ge(row_max_done, NB * FC)
                nc.vector.tensor_reduce(amax[:], row_max[:], AX.XY, ALU.max).then_inc(max_done, 1)


def ffn_output(nc, ins, hidden, hidden_max, xres, w):
    with ExitStack() as ctx:
        m = Pool(nc, ctx, "output")
        scale, back = m.sbuf("scale", [P, 1]), m.sbuf("back", [P, 1])
        hq = w["hq"]
        summed = [m.psum(f"summed{i}") for i in range(2)]
        loaded, step, scaled_done, hq_done, sum_done, bias_done, out_done = (
            m.sem(n) for n in ("loaded", "step", "scaled_done", "hq_done", "sum_done", "bias_done", "out_done"))
        with nc.Block() as block:
            @block.sync
            def _(sp):
                sp.dma_start(w["b_out"], ins["b_out"].partition_broadcast(P)).then_inc(loaded, 16)

            @block.tensor
            def _(pe):
                nc.tensor.sem_inc(out_done, 2)
                with pe.Fori(0, NB) as g:
                    for b in range(B):
                        n = B * g + b + 1
                        pe.wait_ge(hq_done, n)
                        pe.wait_ge(out_done, n)
                        for f in range(FC):
                            last = nc.tensor.matmul(summed[b % 2][:, 0:D], hq[b % 2][:, f, :], w["w_out"][:, f, :],
                                                    start=f == 0, stop=f == FC - 1)
                        last.then_inc(sum_done, 1)

            @block.gpsimd
            def _(pool):
                pool.wait_ge(loaded, 16)
                with pool.Fori(0, NB) as g:
                    for b in range(B):
                        x = xres[:, bass.ds(g, 1), b, :].rearrange("p g d -> p (g d)")
                        nc.gpsimd.tensor_tensor(x, x, w["b_out"], ALU.add).then_inc(bias_done, 1)

            @block.vector
            def _(dve):
                range_scale(nc, dve, hidden_max, scale, back, step, 32767.0)

                def quantize(n, g, b):
                    nc.vector.tensor_scalar(hq[b % 2], hidden[:, :, bass.ds(g * 4 * P + b * P, P)], scale[:], 32767.0,
                                            ALU.mult, ALU.min).then_inc(scaled_done, 1)
                    dve.wait_ge(scaled_done, n)
                    nc.vector.tensor_scalar(hq[b % 2], hq[b % 2], ROUND, ROUND, ALU.add, ALU.subtract).then_inc(hq_done, 1)

                def finish(n, g, b):
                    x = xres[:, bass.ds(g, 1), b, :].rearrange("p g d -> p (g d)")
                    dve.wait_ge(bias_done, n)
                    dve.wait_ge(sum_done, n)
                    nc.vector.scalar_tensor_tensor(x, summed[b % 2][:, 0:D], back[:], x, ALU.mult, ALU.add).then_inc(out_done, 1)
                quantize(1, 0, 0)
                quantize(2, 0, 1)
                with dve.Fori(0, NB - 1) as g:
                    for b in range(B):
                        n = B * g + b + 1
                        finish(n, g, b)
                        quantize(n + 2, g + (b + 2) // B, (b + 2) % B)
                for b in range(B):
                    finish(NT - B + 1 + b, NB - 1, b)
                    if b + 2 < B:
                        quantize(NT - B + 3 + b, NB - 1, b + 2)


def in_steps(eng, stages, groups=NB):
    def group(g, inside):
        for b in range(B):
            for stage, lag in stages:
                ahead = (b - lag) // B
                if inside(ahead):
                    stage(g + ahead, (b - lag) % B)
    group(0, lambda ahead: ahead >= 0)
    with eng.Fori(1, groups) as g:
        group(g, lambda ahead: True)
    group(groups, lambda ahead: ahead < 0)


def tile_of(tensor, g, b):
    return tensor[:, bass.ds(g, 1), b, :].rearrange("p g d -> p (g d)")


def prepare_attention(nc, ins, w):
    with ExitStack() as ctx:
        m = Pool(nc, ctx, "heads")
        wk, wv = m.sbuf("wk", [P, KC, D]), m.sbuf("wv", [P, KC, D])
        bk, bv = m.sbuf("bk", [P, KC]), m.sbuf("bv", [P, D])
        head_mask, pair_mask = m.sbuf("head_mask", [P, 8]), m.sbuf("pair_mask", [P, 2])
        kT = m.sbuf("kT", [P, KC, B * S])
        twice = m.sbuf("twice", [P, KC, B, 2, S])
        v = m.sbuf("v", [P, B, D])
        mask_int = m.sbuf("mask_int", [P, NB, B, S], I32)
        k_sum = [m.psum(f"k_sum{c}") for c in range(KC)]
        v_sum = [m.psum(f"v_sum{b}") for b in range(B)]
        loaded, masks, k_done, v_done, kT_done, doubled, step = (
            m.sem(n) for n in ("loaded", "masks", "k_done", "v_done", "kT_done", "doubled", "step"))
        loads = ((w["ctxT"], "ctxT"), (wk, "wk"), (wv, "wv"), (bk, "bk"), (w["wq"], "wq_k"), (w["wo"], "wo_k"), (w["bq"], "bq"))
        with nc.Block() as block:
            @block.sync
            def _(sp):
                for dst, src in loads:
                    sp.dma_start(dst[:], ins[src]).then_inc(loaded, 16)
                sp.dma_start(bv[:], ins["bv"].partition_broadcast(P)).then_inc(loaded, 16)
                sp.dma_start(w["bo_heads"][:], ins["bo_k"].partition_broadcast(P)).then_inc(loaded, 16)
                for b in range(B):
                    sp.dma_start(mask_int[:, :, b, :], ins["mask"][b].rearrange("(g p) s -> p g s", p=P)).then_inc(loaded, 16)
                    sp.dma_start(w["group_prob"][:, :, b, :], ins["fside"][b].rearrange("(g p) s -> p g s", p=P)).then_inc(loaded, 16)

            @block.gpsimd
            def _(pool):
                nc.gpsimd.memset(head_mask[:], 1.0).then_inc(masks, 1)
                nc.gpsimd.memset(pair_mask[:], 1.0).then_inc(masks, 1)
                for at, (tile, width, count) in enumerate(((head_mask, DH, 8), (pair_mask, S, 2))):
                    pool.wait_ge(masks, 2 + 2 * at)
                    nc.gpsimd.affine_select(out=tile[:], in_=tile[:], compare_op=ALU.is_ge, fill=0.0, base=0,
                                            pattern=[[-width, count]], channel_multiplier=1).then_inc(masks, 1)
                    pool.wait_ge(masks, 3 + 2 * at)
                    nc.gpsimd.affine_select(out=tile[:], in_=tile[:], compare_op=ALU.is_ge, fill=0.0, base=width - 1,
                                            pattern=[[width, count]], channel_multiplier=-1).then_inc(masks, 1)

            @block.tensor
            def _(pe):
                pe.wait_ge(loaded, 16 * (len(loads) + 2 + 2 * B))
                for c in range(KC):
                    for k in range(KC):
                        last = nc.tensor.matmul(k_sum[c][:, 0:B * S], wk[:, k, P * c:P * c + P], w["ctxT"][:, k, :],
                                                start=k == 0, stop=k == KC - 1)
                    last.then_inc(k_done, 1)
                pe.wait_ge(doubled, 2 * KC)
                for b in range(B):
                    for k in range(KC):
                        last = nc.tensor.matmul(v_sum[b][:, 0:D], twice[:, k, b, :, :].rearrange("p a s -> p (a s)"), wv[:, k, :],
                                                start=k == 0, stop=k == KC - 1)
                    last.then_inc(v_done, 1)

            @block.scalar
            def _(act):
                for c in range(KC):
                    act.wait_ge(k_done, c + 1)
                    nc.scalar.activation(kT[:, c, :], k_sum[c][:, 0:B * S], ACT.Identity, bias=bk[:, c:c + 1]).then_inc(kT_done, 1)

            @block.vector
            def _(dve):
                dve.wait_ge(loaded, 16 * (len(loads) + 2 + 2 * B))
                for k in range(KC):
                    for a in range(2):
                        nc.vector.tensor_copy(twice[:, k, :, a, :], w["ctxT"][:, k, :].rearrange("p (b s) -> p b s", b=B)).then_inc(doubled, 1)
                nc.vector.tensor_scalar(w["neg"][:], mask_int[:], 1.0, 1e9, ALU.subtract, ALU.mult).then_inc(step, 1)
                nc.vector.tensor_scalar(w["bq"][:], w["bq"][:], DH ** -0.5, None, ALU.mult).then_inc(step, 1)
                dve.wait_ge(masks, 6)
                for c in range(KC):
                    dve.wait_ge(kT_done, c + 1)
                    for b in range(B):
                        nc.vector.tensor_tensor(w["keys"][:, c, b, :, :],
                                                kT[:, c, S * b:S * b + S].unsqueeze(1).broadcast_to([P, 8, S]),
                                                head_mask[:].unsqueeze(2).broadcast_to([P, 8, S]), ALU.mult).then_inc(step, 1)
                for b in range(B):
                    dve.wait_ge(v_done, b + 1)
                    nc.vector.tensor_tensor(v[:, b, :], v_sum[b][:, 0:D], bv[:], ALU.add).then_inc(step, 1)
                dve.wait_ge(step, 2 + KC * B + B)
                for b in range(B):
                    nc.vector.tensor_tensor(w["values"][:, b, :].rearrange("p (n a d) -> p n a d", a=2, d=DH),
                                            v[:, b, :].rearrange("p (n a d) -> p n a d", a=2, d=DH),
                                            pair_mask[:].unsqueeze(1).unsqueeze(3).broadcast_to([P, H // 2, 2, DH]), ALU.mult).then_inc(step, 1)
                dve.wait_ge(step, 2 + KC * B + 2 * B)


def queries(nc, xres, q_all, w):
    with ExitStack() as ctx:
        m = Pool(nc, ctx, "query")
        norm = norm_memory(m)
        xn = [m.sbuf(f"xn{i}", [P, D]) for i in range(2)]
        xT = [m.sbuf(f"xT{i}", [P, KC, B * P]) for i in range(2)]
        turned = [m.psum(f"turned{i}") for i in range(2)]
        summed = [m.psum(f"summed{i}") for i in range(2)]
        xn_done, turned_done, xT_done, sum_done, q_done = (
            m.sem(n) for n in ("xn_done", "turned_done", "xT_done", "sum_done", "q_done"))
        with nc.Block() as block:
            @block.tensor
            def _(pe):
                nc.tensor.sem_inc(xT_done, 2)
                nc.tensor.sem_inc(q_done, 2)
                with pe.Fori(0, NB // 2) as i:
                    for at in range(2):
                        g = 2 * i + at
                        for b in range(B):
                            pe.wait_ge(xn_done, B * g + b + 1)
                            pe.wait_ge(xT_done, B * g + b + 1)
                            for c in range(KC):
                                last = nc.tensor.transpose(turned[b % 2][:, P * c:P * c + P], xn[b % 2][:, P * c:P * c + P], w["ident"][:])
                            last.then_inc(turned_done, 1)
                        pe.wait_ge(xT_done, B * g + B + 2)
                        for c in range(KC):
                            pe.wait_ge(q_done, KC * g + c + 1)
                            for k in range(KC):
                                last = nc.tensor.matmul(summed[c][:], w["wq"][:, k, P * c:P * c + P], xT[at][:, k, :],
                                                        start=k == 0, stop=k == KC - 1)
                            last.then_inc(sum_done, 1)

            @block.scalar
            def _(act):
                act.wait_ge(norm["eps_done"], 1)
                with act.Fori(0, NB // 2) as i:
                    for at in range(2):
                        g = 2 * i + at
                        for b in range(B):
                            norm_scalar(nc, act, norm, B * g + b + 1)
                            act.wait_ge(turned_done, B * g + b + 1)
                            nc.scalar.activation(xT[at][:, :, P * b:P * b + P], turned[b % 2][:, 0:D].rearrange("p (c n) -> p c n", c=KC),
                                                 ACT.Copy).then_inc(xT_done, 1)
                        for c in range(KC):
                            act.wait_ge(sum_done, KC * g + c + 1)
                            nc.scalar.activation(q_all[:, c, bass.ds(g * B * P, B * P)], summed[c][:], ACT.Identity,
                                                 bias=w["bq"][:, c:c + 1], scale=DH ** -0.5).then_inc(q_done, 1)

            @block.vector
            def _(dve):
                nc.vector.memset(norm["eps"][:], EPS).then_inc(norm["eps_done"], 1)

                def normalize(g, b):
                    norm_vector(nc, dve, norm, B * g + b + 1, tile_of(xres, g, b), xn[b % 2][:]).then_inc(xn_done, 1)
                for b in range(2):
                    normalize(0, b)
                for b in range(2, B):
                    dve.wait_ge(turned_done, b - 1)
                    normalize(0, b)
                with dve.Fori(1, NB) as g:
                    for b in range(B):
                        dve.wait_ge(turned_done, B * g + b - 1)
                        normalize(g, b)


def attention(nc, xres, q_all, w):
    with ExitStack() as ctx:
        m = Pool(nc, ctx, "attn")
        q = [m.sbuf(f"q{i}", [P, KC, P]) for i in range(2)]
        probs = [m.sbuf(f"probs{i}", [P, H, S]) for i in range(2)]
        weighted = [m.sbuf(f"weighted{i}", [P, H, S]) for i in range(2)]
        pT = m.sbuf("pT", [P, 8, P])
        mixedT = [m.sbuf(f"mixedT{i}", [P, KC, P]) for i in range(2)]
        high, total, inv = (([m.sbuf(f"{n}{i}", [P, H]) for i in range(2)]) for n in ("high", "total", "inv"))
        scores = [[m.psum(f"scores{i}{c}") for c in range(KC)] for i in range(2)]
        turned = [m.psum(f"turned{i}") for i in range(2)]
        mixed, y = m.psum("mixed"), m.psum("y")
        (q_ready, scores_done, added, high_done, shifted, exp_done, total_done, inv_done, grouped, weighted_done,
         turned_done, pT_done, mixed_done, mixedT_done, y_done, bias_done, out_done) = (m.sem(n) for n in (
             "q_ready", "scores_done", "added", "high_done", "shifted", "exp_done", "total_done", "inv_done", "grouped",
             "weighted_done", "turned_done", "pT_done", "mixed_done", "mixedT_done", "y_done", "bias_done", "out_done"))
        number = lambda g, b: B * g + b + 1
        with nc.Block() as block:
            @block.tensor
            def _(pe):
                nc.tensor.sem_inc(added, 2)
                nc.tensor.sem_inc(pT_done, 2)
                nc.tensor.sem_inc(mixedT_done, 1)
                nc.tensor.sem_inc(out_done, 1)

                def score(g, b):
                    pe.wait_ge(q_ready, number(g, b))
                    pe.wait_ge(added, number(g, b))
                    for c in range(KC):
                        last = nc.tensor.matmul(scores[b % 2][c][:], q[b % 2][:, c, :], w["keys"][:, c, b, :, :].rearrange("p h s -> p (h s)"),
                                                start=True, stop=True)
                    last.then_inc(scores_done, 1)

                def turn(g, b):
                    n = number(g, b)
                    pe.wait_ge(weighted_done, n + 2)
                    for half in range(2):
                        pe.wait_ge(pT_done, 2 * n + half - 1)
                        for c in range(4):
                            heads = slice(8 * half + 2 * c, 8 * half + 2 * c + 2)
                            last = nc.tensor.transpose(turned[half][:, P * c:P * c + P],
                                                       weighted[b % 2][:, heads, :].rearrange("p h s -> p (h s)"), w["ident"][:])
                        last.then_inc(turned_done, 1)

                def mix(g, b):
                    n = number(g, b)
                    pe.wait_ge(mixedT_done, n)
                    pe.wait_ge(pT_done, 2 * n + 2)
                    for c in range(8):
                        rows = slice(32 * (c % 4), 32 * (c % 4) + 32)
                        last = nc.tensor.matmul(mixed[rows, P * (c // 4):P * (c // 4) + P], w["values"][:, b, 32 * c:32 * c + 32],
                                                pT[:, c, :], start=True, stop=True)
                    last.then_inc(mixed_done, 1)

                def project(g, b):
                    n = number(g, b)
                    pe.wait_ge(mixedT_done, n + 1)
                    pe.wait_ge(out_done, n)
                    for c in range(KC):
                        last = nc.tensor.matmul(y[:, 0:D], mixedT[b % 2][:, c, :], w["wo"][:, c, :], start=c == 0, stop=c == KC - 1)
                    last.then_inc(y_done, 1)
                in_steps(pe, [(score, 0), (turn, 2), (project, 3), (mix, 2)])

            @block.scalar
            def _(act):
                nc.scalar.sem_inc(scores_done, 2)
                nc.scalar.sem_inc(mixed_done, 1)

                def fetch(g, b):
                    n = number(g, b)
                    act.wait_ge(scores_done, n)
                    nc.scalar.activation(q[b % 2][:], q_all[:, :, bass.ds(g * B * P + P * b, P)], ACT.Copy).then_inc(q_ready, 1)

                def exps(g, b):
                    act.wait_ge(shifted, number(g, b))
                    nc.scalar.activation(probs[b % 2][:], probs[b % 2][:], ACT.Exp).then_inc(exp_done, 1)

                def keep_turned(g, b):
                    n = number(g, b)
                    act.wait_ge(mixed_done, n)
                    for half in range(2):
                        act.wait_ge(turned_done, 2 * n + 3 + half)
                        nc.scalar.activation(pT[:, 4 * half:4 * half + 4, :].rearrange("p c n -> p (c n)"), turned[half][:],
                                             ACT.Copy).then_inc(pT_done, 1)

                def keep_mixed(g, b):
                    act.wait_ge(mixed_done, number(g, b) + 1)
                    nc.scalar.activation(mixedT[b % 2][:].rearrange("p c n -> p (c n)"), mixed[:, 0:D], ACT.Copy).then_inc(mixedT_done, 1)
                in_steps(act, [(exps, 1), (fetch, 0), (keep_turned, 2), (keep_mixed, 2)])

            @block.vector
            def _(dve):
                nc.vector.sem_inc(weighted_done, 2)

                def shift(g, b):
                    n = number(g, b)
                    s = b % 2
                    dve.wait_ge(weighted_done, n)
                    dve.wait_ge(scores_done, n + 2)
                    for c in range(KC):
                        last = nc.vector.tensor_tensor(probs[s][:, 8 * c:8 * c + 8, :], scores[s][c][:].rearrange("p (h s) -> p h s", s=S),
                                                       tile_of(w["neg"], g, b).unsqueeze(1).broadcast_to([P, 8, S]), ALU.add)
                    last.then_inc(added, 1)
                    dve.wait_ge(added, n + 2)
                    nc.vector.tensor_reduce(high[s][:], probs[s][:], AX.X, ALU.max).then_inc(high_done, 1)
                    dve.wait_ge(high_done, n)
                    nc.vector.tensor_tensor(probs[s][:], probs[s][:], high[s][:].unsqueeze(2).broadcast_to([P, H, S]),
                                            ALU.subtract).then_inc(shifted, 1)

                def sums(g, b):
                    n = number(g, b)
                    dve.wait_ge(exp_done, n)
                    nc.vector.tensor_reduce(total[b % 2][:], probs[b % 2][:], AX.X, ALU.add).then_inc(total_done, 1)
                    dve.wait_ge(total_done, n)
                    nc.vector.reciprocal(inv[b % 2][:], total[b % 2][:]).then_inc(inv_done, 1)

                def finish(g, b):
                    n = number(g, b)
                    dve.wait_ge(bias_done, n)
                    dve.wait_ge(y_done, n)
                    nc.vector.tensor_tensor(tile_of(xres, g, b), y[:, 0:D], tile_of(xres, g, b), ALU.add).then_inc(out_done, 1)
                in_steps(dve, [(shift, 0), (sums, 1), (finish, 3)])

            @block.gpsimd
            def _(pool):
                nc.gpsimd.sem_inc(turned_done, 4)

                def weigh(g, b):
                    n = number(g, b)
                    s = b % 2
                    x = tile_of(xres, g, b)
                    nc.gpsimd.tensor_tensor(x, x, w["bo_heads"][:], ALU.add).then_inc(bias_done, 1)
                    pool.wait_ge(exp_done, n)
                    pool.wait_ge(turned_done, 2 * n)
                    nc.gpsimd.tensor_tensor(weighted[s][:], probs[s][:],
                                            tile_of(w["group_prob"], g, b).unsqueeze(1).broadcast_to([P, H, S]), ALU.mult).then_inc(grouped, 1)
                    pool.wait_ge(grouped, n)
                    pool.wait_ge(inv_done, n)
                    nc.gpsimd.tensor_tensor(weighted[s][:], weighted[s][:], inv[s][:].unsqueeze(2).broadcast_to([P, H, S]),
                                            ALU.mult).then_inc(weighted_done, 1)
                in_steps(pool, [(weigh, 1)])



def route(nc, ins, xres, xn, slot, expert, prob, slots_x, w):
    with ExitStack() as ctx:
        m = Pool(nc, ctx, "route")
        norm = norm_memory(m)
        sw, sb = m.sbuf("sw", [P, KC, E]), m.sbuf("sb", [P, E])
        xn_tile = [m.sbuf(f"xn_tile{i}", [P, D]) for i in range(2)]
        xT = [m.sbuf(f"xT{i}", [P, KC, P]) for i in range(2)]
        before, ones = m.sbuf("before", [P, P]), m.sbuf("ones", [P, P])
        down, tile_no = m.sbuf("down", [P, E]), m.sbuf("tile_no", [P, SLOT_TILES])
        number_int = m.sbuf("number_int", [P, SLOT_TILES], I32)
        logits, exps, picked = (m.sbuf(n, [P, NT, E]) for n in ("logits", "exps", "picked"))
        one_hot, upto = m.sbuf("one_hot", [P, NT, E]), m.sbuf("upto", [P, NT, E])
        top, total, pick = (m.sbuf(n, [P, NT]) for n in ("top", "total", "pick"))
        tiles, tile_end, first = (m.sbuf(n, [P, E]) for n in ("tiles", "tile_end", "first"))
        ended = m.sbuf("ended", [P, SLOT_TILES, E])
        expert_f = m.sbuf("expert_f", [P, SLOT_TILES])
        slot_f = m.sbuf("slot_f", [P, NT])
        zero = m.sbuf("zero", [P, D])
        turned = [m.psum(f"turned{i}") for i in range(2)]
        summed = [m.psum(f"summed{i}") for i in range(2)]
        rank, count = m.psum("rank"), m.psum("count")
        loaded, zeroed, filled, const, xn_done, turned_done, xT_done, sum_done, logits_done, step, exp_done, counted = (
            m.sem(n) for n in ("loaded", "zeroed", "filled", "const", "xn_done", "turned_done", "xT_done", "sum_done", "logits_done", "step",
                               "exp_done", "counted"))
        with nc.Block() as block:
            @block.sync
            def _(sp):
                sp.dma_start(sw[:], ins["switch_w"]).then_inc(loaded, 16)
                sp.dma_start(sb[:], ins["switch_b"].partition_broadcast(P)).then_inc(loaded, 16)
                sp.wait_ge(zeroed, 1)
                with sp.Fori(0, SLOT_TILES) as j:
                    sp.dma_start(slots_x[bass.ds(j * P, P), :], zero[:]).then_inc(filled, 16)
                for e in range(E):
                    sp.dma_start(w["w1"][:, e, :, :], ins["w1"][e].rearrange("(c p) n -> p c n", p=P)).then_inc(w["loaded"], 16)
                for e in range(E):
                    sp.dma_start(w["w2"][:, e, :, :], ins["w2"][e].rearrange("(f p) n -> p f n", p=P)).then_inc(w["loaded"], 16)
                sp.wait_ge(filled, 16 * SLOT_TILES)

            @block.gpsimd
            def _(pool):
                nc.gpsimd.memset(zero[:], 0.0).then_inc(zeroed, 1)
                nc.gpsimd.memset(before[:], 1.0).then_inc(const, 1)
                nc.gpsimd.memset(ones[:], 1.0).then_inc(const, 1)
                nc.gpsimd.iota(number_int[:], [[1, SLOT_TILES]], base=0, channel_multiplier=0).then_inc(const, 1)
                pool.wait_ge(const, 3)
                nc.gpsimd.affine_select(out=before[:], in_=before[:], compare_op=ALU.is_gt, fill=0.0, base=0,
                                        pattern=[[1, P]], channel_multiplier=-1).then_inc(const, 1)
                nc.gpsimd.tensor_copy(tile_no[:], number_int[:]).then_inc(const, 1)
                for e in range(E):
                    nc.gpsimd.memset(down[:, e:e + 1], float(E - e)).then_inc(const, 1)

            @block.tensor
            def _(pe):
                nc.tensor.sem_inc(xT_done, 2)
                nc.tensor.sem_inc(logits_done, 2)
                pe.wait_ge(loaded, 32)

                def turn(g, b):
                    n = B * g + b + 1
                    pe.wait_ge(xn_done, n)
                    pe.wait_ge(xT_done, n)
                    for c in range(KC):
                        last = nc.tensor.transpose(turned[b % 2][:, P * c:P * c + P], xn_tile[b % 2][:, P * c:P * c + P], w["ident"][:])
                    last.then_inc(turned_done, 1)

                def router(g, b):
                    n = B * g + b + 1
                    pe.wait_ge(xT_done, n + 2)
                    pe.wait_ge(logits_done, n)
                    for c in range(KC):
                        last = nc.tensor.matmul(summed[b % 2][:, 0:E], xT[b % 2][:, c, :], sw[:, c, :], start=c == 0, stop=c == KC - 1)
                    last.then_inc(sum_done, 1)
                in_steps(pe, [(turn, 0), (router, 1)])
                pe.wait_ge(step, 6)
                pe.wait_ge(const, 5 + E)
                chosen = one_hot[:].rearrange("p n e -> p (n e)")
                nc.tensor.matmul(rank[:, 0:NT * E], before[:], chosen, start=True, stop=True)
                nc.tensor.matmul(count[:, 0:NT * E], ones[:], chosen, start=True, stop=True).then_inc(counted, 1)

            @block.scalar
            def _(act):
                act.wait_ge(norm["eps_done"], 1)

                nc.scalar.sem_inc(sum_done, 2)

                def deviation(g, b):
                    norm_scalar(nc, act, norm, B * g + b + 1)

                def keep(g, b):
                    n = B * g + b + 1
                    act.wait_ge(sum_done, n)
                    act.wait_ge(turned_done, n + 2)
                    nc.scalar.activation(xT[b % 2][:].rearrange("p c n -> p (c n)"), turned[b % 2][:, 0:D], ACT.Copy).then_inc(xT_done, 1)
                in_steps(act, [(deviation, 0), (keep, 0)])
                act.wait_ge(step, 2)
                nc.scalar.activation(exps[:], logits[:], ACT.Exp).then_inc(exp_done, 1)

            @block.vector
            def _(dve):
                nc.vector.memset(norm["eps"][:], EPS).then_inc(norm["eps_done"], 1)
                nc.vector.sem_inc(turned_done, 2)
                dve.wait_ge(loaded, 32)

                def normalize(g, b):
                    n = B * g + b + 1
                    dve.wait_ge(turned_done, n)
                    norm_vector(nc, dve, norm, n, tile_of(xres, g, b), xn_tile[b % 2][:]).then_inc(xn_done, 1)
                    dve.wait_ge(xn_done, n)
                    nc.vector.tensor_copy(tile_of(xn, g, b), xn_tile[b % 2][:])

                def keep_logits(g, b):
                    n = B * g + b + 1
                    dve.wait_ge(sum_done, n + 2)
                    nc.vector.tensor_tensor(logits[:, bass.ds(g * B + b, 1), :].rearrange("p n e -> p (n e)"), summed[b % 2][:, 0:E],
                                            sb[:], ALU.add).then_inc(logits_done, 1)
                in_steps(dve, [(normalize, 0), (keep_logits, 1)])

                over_experts = [P, NT, E]

                def then(instruction, n):
                    instruction.then_inc(step, 1)
                    dve.wait_ge(step, n)
                dve.wait_ge(logits_done, NT + 2)
                then(nc.vector.tensor_reduce(top[:], logits[:], AX.X, ALU.max), 1)
                then(nc.vector.tensor_tensor(logits[:], logits[:], top[:].unsqueeze(2).broadcast_to(over_experts), ALU.subtract), 2)
                then(nc.vector.tensor_scalar(picked[:], logits[:], 0.0, None, ALU.is_ge), 3)
                dve.wait_ge(const, 5 + E)
                then(nc.vector.tensor_tensor(picked[:], picked[:], down[:].unsqueeze(1).broadcast_to(over_experts), ALU.mult), 4)
                then(nc.vector.tensor_reduce(pick[:], picked[:], AX.X, ALU.max), 5)
                then(nc.vector.tensor_tensor(one_hot[:], picked[:], pick[:].unsqueeze(2).broadcast_to(over_experts), ALU.is_equal), 6)
                dve.wait_ge(exp_done, 1)
                then(nc.vector.tensor_reduce(total[:], exps[:], AX.X, ALU.add), 7)
                then(nc.vector.reciprocal(prob[:], total[:]), 8)
                dve.wait_ge(counted, 1)
                then(nc.vector.tensor_copy(picked[:].rearrange("p n e -> p (n e)"), count[:, 0:NT * E]), 9)
                nc.vector.memset(exps[:], 1.0).then_inc(step, 1)
                dve.wait_ge(step, 10)
                for e in range(E):
                    nc.vector.tensor_tensor_scan(upto[:, :, e], exps[:, :, e], picked[:, :, e], 0.0, ALU.mult, ALU.add).then_inc(step, 1)
                dve.wait_ge(step, 10 + E)
                k = 10 + E
                then(nc.vector.tensor_scalar(tiles[:], upto[:, NT - 1, :], 1.0 / P, (P - 1) / P - (P - 1) / (2 * P), ALU.mult, ALU.add), k + 1)
                then(nc.vector.tensor_scalar(tiles[:], tiles[:], ROUND, ROUND, ALU.add, ALU.subtract), k + 2)
                then(nc.vector.tensor_tensor_scan(tile_end[:], exps[:, 0, :], tiles[:], 0.0, ALU.mult, ALU.add), k + 3)
                then(nc.vector.tensor_tensor(first[:], tile_end[:], tiles[:], ALU.subtract), k + 4)
                then(nc.vector.tensor_scalar(first[:], first[:], float(P), None, ALU.mult), k + 5)
                then(nc.vector.tensor_tensor(upto[:], upto[:], picked[:], ALU.subtract), k + 6)
                then(nc.vector.tensor_tensor(upto[:], upto[:], first[:].unsqueeze(1).broadcast_to(over_experts), ALU.add), k + 7)
                then(nc.vector.tensor_tensor(upto[:].rearrange("p n e -> p (n e)"), rank[:, 0:NT * E], upto[:].rearrange("p n e -> p (n e)"), ALU.add), k + 8)
                then(nc.vector.tensor_tensor(upto[:], upto[:], one_hot[:], ALU.mult), k + 9)
                then(nc.vector.tensor_reduce(slot_f[:], upto[:], AX.X, ALU.add), k + 10)
                then(nc.vector.tensor_copy(slot[:], slot_f[:]), k + 11)
                then(nc.vector.tensor_tensor(ended[:], tile_no[:].unsqueeze(2).broadcast_to([P, SLOT_TILES, E]),
                                             tile_end[:].unsqueeze(1).broadcast_to([P, SLOT_TILES, E]), ALU.is_ge), k + 12)
                then(nc.vector.tensor_reduce(expert_f[:], ended[:], AX.X, ALU.add), k + 13)
                then(nc.vector.tensor_scalar(expert_f[:], expert_f[:], float(E - 1), None, ALU.min), k + 14)
                then(nc.vector.tensor_copy(expert[:], expert_f[:]), k + 15)


def scatter(nc, xn, slot, slots_x):
    sent = Pool(nc, None, "scatter").sem("sent")
    with nc.Block() as block:
        @block.gpsimd
        def _(pool):
            for n in range(NT):
                nc.gpsimd.indirect_dma_start(slots_x, bass.IndirectOffsetOnAxis(ap=slot[:, n:n + 1], axis=0),
                                             xn[:, n // B, n % B, :], None).then_inc(sent, 16)
            pool.wait_ge(sent, 16 * NT)


def experts(nc, ins, expert, slots_x, slots_y, w):
    with ExitStack() as ctx:
        m = Pool(nc, ctx, "experts")
        x = [m.sbuf(f"x{i}", [P, D]) for i in range(2)]
        xT = m.sbuf("xT", [P, KC, P])
        bias = [m.sbuf(f"bias{i}", [P, FF + D]) for i in range(2)]
        hidden = [m.sbuf(f"hidden{i}", [P, FF]) for i in range(2)]
        hT = m.sbuf("hT", [P, FC, P])
        y = [m.sbuf(f"y{i}", [P, D]) for i in range(2)]
        x_turned, y_sum = m.psum("x_turned"), m.psum("y_sum")
        h_sum = [m.psum(f"h_sum{i}") for i in range(2)]
        h_turned = [m.psum(f"h_turned{i}") for i in range(2)]
        x_in = [m.sem(f"x_in{i}") for i in range(2)]
        bias_in = [m.sem(f"bias_in{i}") for i in range(2)]
        stored = [m.sem(f"stored{i}") for i in range(2)]
        x_turned_done, xT_done, h_sum_done, h_done, gelu_done, h_turned_done, hT_done, y_sum_done, y_done = (
            m.sem(n) for n in ("x_turned_done", "xT_done", "h_sum_done", "h_done", "gelu_done", "h_turned_done", "hT_done",
                               "y_sum_done", "y_done"))
        GROUPS = SLOT_TILES // B
        number = lambda g, b: B * g + b + 1
        seen = lambda g, b: 32 * g + 16 * (b // 2) + 16
        with nc.Block() as block:
            @block.sync
            def _(sp):
                sp.sem_inc(x_turned_done, 2)
                sp.sem_inc(y_done, 2)

                def load(g, b):
                    n = number(g, b)
                    sp.wait_ge(x_turned_done, n)
                    sp.dma_start(x[b % 2][:], slots_x[bass.ds(g * B * P + P * b, P), :]).then_inc(x_in[b % 2], 16)
                    sp.wait_ge(y_done, n)
                    e = sp.value_load(expert[0:1, bass.ds(g * B + b, 1)], min_val=0, max_val=E - 1)
                    sp.dma_start(bias[b % 2][:], ins["b12"][bass.ds(e, 1), :].rearrange("a n -> (a n)").partition_broadcast(P)).then_inc(bias_in[b % 2], 16)

                def store(g, b):
                    sp.wait_ge(y_done, number(g, b) + 2)
                    sp.dma_start(slots_y[bass.ds(g * B * P + P * b, P), :], y[b % 2][:]).then_inc(stored[b % 2], 16)
                in_steps(sp, [(store, 2), (load, 0)], GROUPS)
                for s in range(2):
                    sp.wait_ge(stored[s], 16 * SLOT_TILES // 2 + 16)

            @block.tensor
            def _(pe):
                nc.tensor.sem_inc(xT_done, 1)
                nc.tensor.sem_inc(h_done, 1)
                nc.tensor.sem_inc(hT_done, 2)
                pe.wait_ge(w["loaded"], 16 * 2 * E)

                def up(g, b):
                    n = number(g, b)
                    pe.wait_ge(x_in[b % 2], seen(g, b))
                    pe.wait_ge(xT_done, n)
                    for c in range(KC):
                        last = nc.tensor.transpose(x_turned[:, P * c:P * c + P], x[b % 2][:, P * c:P * c + P], w["ident"][:])
                    last.then_inc(x_turned_done, 1)

                def up_product(g, b):
                    n = number(g, b)
                    e = pe.value_load(expert[0:1, bass.ds(g * B + b, 1)], min_val=0, max_val=E - 1)
                    pe.wait_ge(xT_done, n + 1)
                    pe.wait_ge(h_done, n)
                    for half in range(2):
                        for c in range(KC):
                            last = nc.tensor.matmul(h_sum[half][:], xT[:, c, :],
                                                    w["w1"][:, bass.ds(e, 1), c, 512 * half:512 * half + 512].rearrange("p a n -> p (a n)"),
                                                    start=c == 0, stop=c == KC - 1)
                    last.then_inc(h_sum_done, 1)

                def turn(g, b):
                    n = number(g, b)
                    pe.wait_ge(gelu_done, n)
                    for half in range(2):
                        pe.wait_ge(hT_done, 2 * n - 1 + half)
                        for c in range(4):
                            f = 4 * half + c
                            last = nc.tensor.transpose(h_turned[half][:, P * c:P * c + P], hidden[b % 2][:, P * f:P * f + P], w["ident"][:])
                        last.then_inc(h_turned_done, 1)

                def down_product(g, b):
                    n = number(g, b)
                    e = pe.value_load(expert[0:1, bass.ds(g * B + b, 1)], min_val=0, max_val=E - 1)
                    pe.wait_ge(hT_done, 2 * n + 2)
                    pe.wait_ge(y_done, n + 1)
                    for f in range(FC):
                        last = nc.tensor.matmul(y_sum[:, 0:D], hT[:, f, :], w["w2"][:, bass.ds(e, 1), f, :].rearrange("p a n -> p (a n)"),
                                                start=f == 0, stop=f == FC - 1)
                    last.then_inc(y_sum_done, 1)
                in_steps(pe, [(up, 0), (turn, 1), (up_product, 0), (down_product, 1)], GROUPS)

            @block.scalar
            def _(act):
                nc.scalar.sem_inc(h_sum_done, 1)
                nc.scalar.sem_inc(y_sum_done, 1)

                def keep_x(g, b):
                    n = number(g, b)
                    act.wait_ge(h_sum_done, n)
                    act.wait_ge(x_turned_done, n + 2)
                    nc.scalar.activation(xT[:].rearrange("p c n -> p (c n)"), x_turned[:, 0:D], ACT.Copy).then_inc(xT_done, 1)

                def gelu(g, b):
                    act.wait_ge(h_done, number(g, b) + 1)
                    nc.scalar.activation(hidden[b % 2][:], hidden[b % 2][:], ACT.Gelu_apprx_tanh).then_inc(gelu_done, 1)

                def keep_hidden(g, b):
                    n = number(g, b)
                    act.wait_ge(y_sum_done, n)
                    for half in range(2):
                        act.wait_ge(h_turned_done, 2 * n - 1 + half + 4)
                        nc.scalar.activation(hT[:, 4 * half:4 * half + 4, :].rearrange("p c n -> p (c n)"), h_turned[half][:],
                                             ACT.Copy).then_inc(hT_done, 1)
                in_steps(act, [(keep_x, 0), (keep_hidden, 1), (gelu, 0)], GROUPS)

            @block.vector
            def _(dve):
                nc.vector.sem_inc(h_turned_done, 4)
                for s in range(2):
                    nc.vector.sem_inc(stored[s], 16)

                def add_bias(g, b):
                    n = number(g, b)
                    dve.wait_ge(h_turned_done, 2 * n)
                    dve.wait_ge(bias_in[b % 2], seen(g, b))
                    dve.wait_ge(h_sum_done, n + 1)
                    for half in range(2):
                        at = slice(512 * half, 512 * half + 512)
                        last = nc.vector.tensor_tensor(hidden[b % 2][:, at], h_sum[half][:], bias[b % 2][:, at], ALU.add)
                    last.then_inc(h_done, 1)

                def finish(g, b):
                    dve.wait_ge(stored[b % 2], seen(g, b))
                    dve.wait_ge(y_sum_done, number(g, b) + 1)
                    nc.vector.tensor_tensor(y[b % 2][:], y_sum[:, 0:D], bias[b % 2][:, FF:FF + D], ALU.add).then_inc(y_done, 1)
                in_steps(dve, [(add_bias, 0), (finish, 1)], GROUPS)


def gather(nc, xres, slot, prob, slots_y, out):
    with ExitStack() as ctx:
        m = Pool(nc, ctx, "gather")
        y = m.sbuf("y", [P, NT, D])
        fetched, added, sent = m.sem("fetched"), m.sem("added"), m.sem("sent")
        with nc.Block() as block:
            @block.gpsimd
            def _(pool):
                for n in range(NT):
                    nc.gpsimd.indirect_dma_start(y[:, n, :], None, slots_y,
                                                 bass.IndirectOffsetOnAxis(ap=slot[:, n:n + 1], axis=0)).then_inc(fetched, 16)
                pool.wait_ge(fetched, 16 * NT)

            @block.vector
            def _(dve):
                dve.wait_ge(fetched, 16 * NT)
                for n in range(NT):
                    g, b = n // B, n % B
                    nc.vector.scalar_tensor_tensor(xres[:, g, b, :], y[:, n, :], prob[:, n:n + 1], xres[:, g, b, :],
                                                   ALU.mult, ALU.add).then_inc(added, 1)

            @block.sync
            def _(sp):
                for g in range(NB):
                    sp.wait_ge(added, B * g + B)
                    sp.dma_start(out[:, P * g:P * g + P, :].rearrange("b p d -> p b d"), xres[:, g, :, :]).then_inc(sent, 16)
                sp.wait_ge(sent, 16 * NB)


def build(nc, ins, out):
    gx_scratch = nc.dram_tensor("gx_scratch", (T * B, 4 * D), F32).ap()
    slots_x = nc.dram_tensor("slots_x", (SLOT_TILES * P, D), F32).ap()
    slots_y = nc.dram_tensor("slots_y", (SLOT_TILES * P, D), F32).ap()
    TAKEN.clear()
    with ExitStack() as whole:
        keep = Pool(nc, whole, "w")
        ident = keep.sbuf("ident", [P, P])
        xres = keep.sbuf("xres", [P, NB, B, D])
        with ExitStack() as ffn:
            m = Pool(nc, ffn, "ffn")
            xn = m.sbuf("xn", [P, NB, B, D])
            w = {"ident": ident, "w_in": m.sbuf("w_in", [P, KC, FF], BF16), "back": m.sbuf("back", [P, FC]),
                 "b_in": m.sbuf("b_in", [P, FC])}
            norm_max, hidden_max = m.sbuf("norm_max", [P, 1]), m.sbuf("hidden_max", [P, 1])
            spare = xn[:].rearrange("p g b d -> p (g b d)")
            w_out = spare[:, 0:FC * D].rearrange("p (f n) -> p f n", f=FC)
            hq = [spare[:, (2 + i) * FF:(3 + i) * FF].rearrange("p (f n) -> p f n", f=FC) for i in range(2)]
            with ExitStack() as recurrent:
                a_hist = Pool(nc, recurrent, "a").sbuf("hist", [P, T, 2, B])
                with ExitStack() as ctx:
                    m = Pool(nc, ctx, "rec")
                    r = {"ident": ident, "ctxT": m.sbuf("ctxT", [P, KC, B * S])}
                    for name in ("wa", "wh0", "wi1", "wh1"):
                        r[name] = m.sbuf(name, [P, 2, 4, GATES * 64])
                    for name in ("kp", "woh", "vp"):
                        r[name] = m.sbuf(name, [P, 2, 4, 64])
                    r["wx"] = m.sbuf("wx", [P, KC, 4 * D])
                    r["wx_bias"] = m.sbuf("wx_bias", [P, 4, GATES, 64])
                    r["b1"] = m.sbuf("b1", [P, GATES, 64])
                    r["bo"] = m.sbuf("bo", [P, 64])
                    r["off_rows"] = m.sbuf("off_rows", [P, 1])
                    prepare_scan(nc, ins, r)
                    input_gates(nc, ins["x_steps"], gx_scratch, r)
                    scan(nc, gx_scratch.rearrange("(t b) (j n) -> t b j n", b=B, j=4), a_hist, r)
                quantize_rows(nc, "quant_in", ins["w_in"], w_out, w["back"][:], False)
                turn_first_weight(nc, ins, w_out, w)
                add_attention_and_normalize(nc, ins["x"], a_hist, xres, xn, norm_max, w)
            with ExitStack() as ctx:
                m = Pool(nc, ctx, "ffn")
                hidden = m.sbuf("hidden", [P, FC, B * T])
                ffn_hidden(nc, xn, norm_max, hidden, hidden_max, w)
                back_out = m.sbuf("back_out", [P, FC])
                quantize_rows(nc, "quant_out", ins["w_out"], w_out, back_out[:], True)
                w.update(w_out=w_out, hq=hq, b_out=spare[:, 4 * FF:4 * FF + D])
                ffn_output(nc, ins, hidden, hidden_max, xres, w)
        release_semaphores(nc)
        with ExitStack() as ctx:
            m = Pool(nc, ctx, "heads")
            w = {"ident": ident, "ctxT": m.sbuf("ctxT", [P, KC, B * S]), "wq": m.sbuf("wq", [P, KC, D]), "wo": m.sbuf("wo", [P, KC, D]),
                 "bq": m.sbuf("bq", [P, KC]), "bo_heads": m.sbuf("bo_heads", [P, D]), "neg": m.sbuf("neg", [P, NB, B, S]),
                 "group_prob": m.sbuf("group_prob", [P, NB, B, S]), "keys": m.sbuf("keys", [P, KC, B, 8, S]),
                 "values": m.sbuf("values", [P, B, D])}
            q_all = m.sbuf("q_all", [P, KC, B * T])
            prepare_attention(nc, ins, w)
            queries(nc, xres, q_all, w)
            attention(nc, xres, q_all, w)
        with ExitStack() as ctx:
            m = Pool(nc, ctx, "moe")
            w = {"ident": ident, "w1": m.sbuf("w1", [P, E, KC, FF]), "w2": m.sbuf("w2", [P, E, FC, D]), "loaded": m.sem("loaded")}
            slot = m.sbuf("slot", [P, NT], I32)
            expert = m.sbuf("expert", [P, SLOT_TILES], I32)
            prob = m.sbuf("prob", [P, NT])
            with ExitStack() as routing:
                xn = Pool(nc, routing, "moe").sbuf("xn", [P, NB, B, D])
                route(nc, ins, xres, xn, slot, expert, prob, slots_x, w)
                scatter(nc, xn, slot, slots_x)
            experts(nc, ins, expert, slots_x, slots_y, w)
            gather(nc, xres, slot, prob, slots_y, out)


def lay_out(inputs):
    import numpy as np
    a = {k: np.asarray(v) for k, v in inputs.items()}

    def gate_blocks(rows):
        return rows.reshape((GATES, 4, 64) + rows.shape[1:])[[3, 0, 1, 2]]

    def from_state(weight):
        g = gate_blocks(weight).reshape(GATES, 4, 64, 4, 2, 32)
        return g.transpose(3, 5, 4, 1, 0, 2).reshape(P, 2, 4, GATES * 64)

    def chunked(weight):
        return weight.reshape((-1, P) + weight.shape[1:]).swapaxes(0, 1)

    def bias_blocks(bias):
        return gate_blocks(bias).transpose(1, 0, 2)
    wi0, wo = a["L0_xattn_Wi0"], a["L0_xattn_Wo"]
    out = {
        "x": a["x"],
        "x_steps": a["x"].transpose(1, 0, 2).reshape(T * B, D),
        "ctxT": chunked(a["ctx_1024"].transpose(2, 0, 1).reshape(D, B * S)),
        "ctx_split": chunked(a["ctx_1024"].reshape(B, 2, 32, D).transpose(3, 1, 0, 2).reshape(D, 2, P)),
        "wx": chunked(gate_blocks(wi0[:, :D]).transpose(3, 1, 0, 2).reshape(D, 4 * D)),
        "wa": from_state(wi0[:, D:]),
        "wh0": from_state(a["L0_xattn_Wh0"]),
        "wi1": from_state(a["L0_xattn_Wi1"]),
        "wh1": from_state(a["L0_xattn_Wh1"]),
        "wq": a["L0_xattn_Wq"].reshape(KC, P, 4, 2, 32).transpose(1, 0, 3, 2, 4).reshape(P, KC, 2, P),
        "wo_mixed": chunked(wo[:, :D].T),
        "woh": wo[:, D:].reshape(4, 64, 4, 2, 32).transpose(2, 4, 3, 0, 1).reshape(P, 2, 4, 64),
        "bo": a["L0_xattn_bo"].reshape(4, 64),
        "w_in": chunked(a["L0_ffn_W_in"].T),
        "b_in": a["L0_ffn_b_in"].reshape(FC, P).T,
        "w_out": chunked(a["L0_ffn_W_out"]),
        "b_out": a["L0_ffn_b_out"],
        "wq_k": chunked(a["L1_xattn_wq_k"]), "wk": chunked(a["L1_xattn_wk_k"]), "wv": chunked(a["L1_xattn_wv_k"]),
        "wo_k": chunked(a["L1_xattn_wo_k"]),
        "bq": a["L1_xattn_wq_b"].reshape(KC, P).T, "bk": a["L1_xattn_wk_b"].reshape(KC, P).T,
        "bv": a["L1_xattn_wv_b"], "bo_k": a["L1_xattn_wo_b"],
        "mask": a["mask_BxSxS2_ik1"], "fside": a["fside_BxSxS2_0"],
        "switch_w": chunked(a["L1_ffn_switch_w"]), "switch_b": a["L1_ffn_switch_b"],
        "w1": a["L1_ffn_w1"], "w2": a["L1_ffn_w2"],
        "b12": np.concatenate([a["L1_ffn_b1"], a["L1_ffn_b2"]], axis=1),
    }
    for name in ("bi0", "bh0", "bi1", "bh1"):
        out[name] = bias_blocks(a[f"L0_xattn_{name}"])
    return {k: np.ascontiguousarray(v) for k, v in out.items()}


def kernel(**inputs):
    import concourse.bacc as bacc
    from concourse.bass_utils import run_bass_kernel_spmd
    nc = bacc.Bacc("TRN2", target_bir_lowering=False, num_devices=1)
    arrays = lay_out(inputs)
    ins = {name: nc.dram_tensor(f"in_{name}", a.shape, mybir.dt.from_np(a.dtype), kind="ExternalInput").ap()
           for name, a in arrays.items()}
    out = nc.dram_tensor("out", (B, T, D), F32, kind="ExternalOutput").ap()
    build(nc, ins, out)
    result = run_bass_kernel_spmd(nc, [{f"in_{name}": a for name, a in arrays.items()}], core_ids=[0])
    return result.results[0]["out"]
```
